# Optimizing a Trainium2 kernel written in Bass

```python
import numpy as np
import jax
import jax.numpy as jnp

def _softmax(x, axis=-1):
    return jax.nn.softmax(x, axis=axis)

def _gelu(x):
    return jax.nn.gelu(x, approximate=True)

def _silu(x):
    return jax.nn.silu(x)

def _sigmoid(x):
    return jax.nn.sigmoid(x)

def _layernorm(x, axis=-1, eps=1e-05):
    m = jnp.mean(x, axis=axis, keepdims=True)
    v = jnp.var(x, axis=axis, keepdims=True)
    return (x - m) / jnp.sqrt(v + eps)

def _scatter_add(tgt, idx, src, axis=0):
    return tgt.at[idx].add(src)

def _segment_sum(src, seg, n):
    return jax.ops.segment_sum(src, seg, n)
kernel_name = 'mk_macaron_d1_jaxref_r8_aa5e2f'

def setup_inputs(seed: int=0):
    np.random.seed(seed)
    _w = jnp.asarray

    def _L0_attn_setup():
        import jax, jax.numpy as jnp
        import numpy as np
        B, L, D, S, K, FF = (2, 512, 128, 16, 3, 336)
        EPS = 1e-06

        def rmsnorm(x, w):
            var = jnp.mean(x * x, axis=-1, keepdims=True)
            return x * jax.lax.rsqrt(var + EPS) * w
        key = jax.random.key(seed)
        ks = jax.random.split(key, 12)
        return {'u': jax.random.normal(ks[0], (B, L, D), jnp.float32), 'pre_norm_w': jnp.ones((D,), jnp.float32), 'in_proj_w': jax.random.normal(ks[1], (3 * D, D), jnp.float32) * D ** (-0.5), 'short_w': jax.random.normal(ks[2], (3 * D, 1, K), jnp.float32) * 0.3, 'short_b': jax.random.normal(ks[3], (3 * D,), jnp.float32) * 0.02, 'log_poles': -(jax.random.uniform(ks[4], (D, S, 1), jnp.float32) * 0.3 + 0.001), 'residues': jax.random.normal(ks[5], (D, S), jnp.float32) * S ** (-0.5), 'D_skip': jax.random.normal(ks[6], (D,), jnp.float32) * 0.02, 'out_proj_w': jax.random.normal(ks[7], (D, D), jnp.float32) * D ** (-0.5), 'post_norm_w': jnp.ones((D,), jnp.float32), 'l1_w': jax.random.normal(ks[8], (FF, D), jnp.float32) * D ** (-0.5), 'l2_w': jax.random.normal(ks[9], (FF, D), jnp.float32) * D ** (-0.5), 'l3_w': jax.random.normal(ks[10], (D, FF), jnp.float32) * FF ** (-0.5)}
    _L0_attn_in = _L0_attn_setup()

    def _L0_ffn_setup():
        import jax, jax.numpy as jnp
        import numpy as np
        EMB = 128
        FF = 4 * EMB

        def _ternary(w):
            scale = jnp.maximum(jnp.mean(jnp.abs(w)), 1e-08)
            w_t = jnp.clip(jnp.round(w / scale), -1.0, 1.0)
            return w + jax.lax.stop_gradient(w_t - w)
        key = jax.random.key(seed)
        kx, k1, k2, kb1, kb2 = jax.random.split(key, 5)
        x = jax.random.normal(kx, (4, 256, EMB), dtype=jnp.float32)
        lim1 = 1.0 / np.sqrt(EMB)
        lim2 = 1.0 / np.sqrt(FF)
        W1 = jax.random.uniform(k1, (FF, EMB), jnp.float32, -lim1, lim1)
        b1 = jax.random.uniform(kb1, (FF,), jnp.float32, -lim1, lim1)
        W2 = jax.random.uniform(k2, (EMB, FF), jnp.float32, -lim2, lim2)
        b2 = jax.random.uniform(kb2, (EMB,), jnp.float32, -lim2, lim2)
        return {'x': x, 'W1': W1, 'b1': b1, 'W2': W2, 'b2': b2}
    _L0_ffn_in = _L0_ffn_setup()
    _d = {'L0_attn_u': _L0_attn_in['u'], 'L0_attn_pre_norm_w': _L0_attn_in['pre_norm_w'], 'L0_attn_in_proj_w': _L0_attn_in['in_proj_w'], 'L0_attn_short_w': _L0_attn_in['short_w'], 'L0_attn_short_b': _L0_attn_in['short_b'], 'L0_attn_log_poles': _L0_attn_in['log_poles'], 'L0_attn_residues': _L0_attn_in['residues'], 'L0_attn_D_skip': _L0_attn_in['D_skip'], 'L0_attn_out_proj_w': _L0_attn_in['out_proj_w'], 'L0_attn_post_norm_w': _L0_attn_in['post_norm_w'], 'L0_attn_l1_w': _L0_attn_in['l1_w'], 'L0_attn_l2_w': _L0_attn_in['l2_w'], 'L0_attn_l3_w': _L0_attn_in['l3_w'], 'L0_ffn_W1': _L0_ffn_in['W1'], 'L0_ffn_b1': _L0_ffn_in['b1'], 'L0_ffn_W2': _L0_ffn_in['W2'], 'L0_ffn_b2': _L0_ffn_in['b2']}
    _x0 = _d['L0_attn_u']
    _d['L0_attn_u'] = jax.random.normal(jax.random.fold_in(jax.random.key(seed), 1), (8, 1024, 128), dtype=_x0.dtype)
    del _x0
    return _d

def reference(L0_attn_u, L0_attn_pre_norm_w, L0_attn_in_proj_w, L0_attn_short_w, L0_attn_short_b, L0_attn_log_poles, L0_attn_residues, L0_attn_D_skip, L0_attn_out_proj_w, L0_attn_post_norm_w, L0_attn_l1_w, L0_attn_l2_w, L0_attn_l3_w, L0_ffn_W1, L0_ffn_b1, L0_ffn_W2, L0_ffn_b2):

    def _L0_attn_ref(u, pre_norm_w, in_proj_w, short_w, short_b, log_poles, residues, D_skip, out_proj_w, post_norm_w, l1_w, l2_w, l3_w):
        import jax, jax.numpy as jnp
        import numpy as np
        B, L, D, S, K, FF = (2, 512, 128, 16, 3, 336)
        EPS = 1e-06

        def rmsnorm(x, w):
            var = jnp.mean(x * x, axis=-1, keepdims=True)
            return x * jax.lax.rsqrt(var + EPS) * w
        Lc = u.shape[1]
        z = rmsnorm(u, pre_norm_w) @ in_proj_w.T
        zc = z.transpose(0, 2, 1)
        z_pre = jax.lax.conv_general_dilated(zc, short_w, window_strides=(1,), padding=[(K - 1, 0)], dimension_numbers=('NCH', 'OIH', 'NCH'), feature_group_count=3 * D)
        z_pre = z_pre + short_b[None, :, None]
        x2, x1, v = jnp.split(z_pre, 3, axis=1)
        t = jnp.arange(Lc, dtype=jnp.float32)
        h = jnp.sum(residues[:, :, None] * jnp.exp(log_poles * t[None, None, :]), axis=1)
        xv = x1 * v
        n = 2 * Lc
        Xf = jnp.fft.rfft(xv, n=n)
        Hf = jnp.fft.rfft(h, n=n)
        yconv = jnp.fft.irfft(Xf * Hf[None], n=n)[..., :Lc]
        y = (yconv + xv * D_skip[None, :, None]) * x2
        y = y.transpose(0, 2, 1)
        y = y @ out_proj_w.T + u
        zm = rmsnorm(y, post_norm_w)
        mlp = jax.nn.gelu(zm @ l1_w.T) * (zm @ l2_w.T) @ l3_w.T
        return y + mlp

    def _L0_ffn_ref(x, W1, b1, W2, b2):
        import jax, jax.numpy as jnp
        import numpy as np
        EMB = 128
        FF = 4 * EMB

        def _ternary(w):
            scale = jnp.maximum(jnp.mean(jnp.abs(w)), 1e-08)
            w_t = jnp.clip(jnp.round(w / scale), -1.0, 1.0)
            return w + jax.lax.stop_gradient(w_t - w)
        h = jnp.einsum('bsd,fd->bsf', x, _ternary(W1)) + b1
        h = jax.nn.gelu(h, approximate=False)
        out = jnp.einsum('bsf,df->bsd', h, _ternary(W2)) + b2
        return out
    x = L0_attn_u
    x = x + 0.5 * _L0_ffn_ref(_layernorm(x, axis=-1), L0_ffn_W1, L0_ffn_b1, L0_ffn_W2, L0_ffn_b2)
    x = x + _L0_attn_ref(_layernorm(x, axis=-1), L0_attn_pre_norm_w, L0_attn_in_proj_w, L0_attn_short_w, L0_attn_short_b, L0_attn_log_poles, L0_attn_residues, L0_attn_D_skip, L0_attn_out_proj_w, L0_attn_post_norm_w, L0_attn_l1_w, L0_attn_l2_w, L0_attn_l3_w)
    x = x + 0.5 * _L0_ffn_ref(_layernorm(x, axis=-1), L0_ffn_W1, L0_ffn_b1, L0_ffn_W2, L0_ffn_b2)
    return x

_drawn_inputs = setup_inputs


def setup_inputs(seed=0):
    import zlib

    import numpy as np

    out = dict(_drawn_inputs(seed))
    spreads = {'L0_attn_pre_norm_w': (1.0, 0.6), 'L0_attn_post_norm_w': (1.0, 0.6)}
    factors = {'L0_attn_in_proj_w': 3.145,
     'L0_attn_short_w': 4.038,
     'L0_attn_short_b': 8.0,
     'L0_attn_log_poles': 4.922,
     'L0_attn_residues': 2.965,
     'L0_attn_D_skip': 8.0,
     'L0_attn_out_proj_w': 3.951,
     'L0_attn_l1_w': 35.436,
     'L0_attn_l2_w': 24.399,
     'L0_attn_l3_w': 25.096,
     'L0_ffn_b1': 8.0,
     'L0_ffn_b2': 64.0}
    for name, (base, spread) in spreads.items():
        noise = np.random.default_rng([zlib.crc32(name.encode()), seed]).standard_normal(out[name].shape)
        drawn = base * np.exp(spread * noise) if base else spread * noise
        out[name] = jnp.asarray(drawn.astype(out[name].dtype))
    for name, factor in factors.items():
        out[name] = (out[name] * factor).astype(out[name].dtype)
    return out
```

```python
from contextlib import ExitStack

import concourse.bass as bass
from concourse import mybir

F32 = mybir.dt.float32
F16 = mybir.dt.float16
BF16 = mybir.dt.bfloat16
ALU = mybir.AluOpType
ACT = mybir.ActivationFunctionType
AX_X = mybir.AxisListType.X

P = 128
B, L, D = 8, 1024, 128
FF = 512
NF = FF // P
S = 16
K = 3
GF = 336
GP = 112
NG = GF // GP
TILES = B * L // P
CH = L // P
T4 = 4
BT = T4 * P
NB = TILES // T4
DG = P // S
NGR = D // DG
TAB = NGR * P
HW = 2 * P
LN_EPS = 1e-5
RMS_EPS = 1e-6
MIX_C = 2 * D


def after(eng, sem, count):
    if not (isinstance(count, int) and count <= 0):
        eng.wait_ge(sem, count)


def each_block(eng, step, peel_front, peel_back=2):
    for i in range(peel_front):
        step(i, i % 2, i)
    with eng.Fori(peel_front // 2, (NB - peel_back) // 2) as pair:
        step(pair * 2, 0, None)
        step(pair * 2 + 1, 1, None)
    for i in range(NB - peel_back, NB):
        step(i, i % 2, i)


def macaron_kernel(nc, x, w1t, b1c, w2t, bias_rows, pre_w, wint, short_rows, short_bc, poles, residues,
                   dskip, wot, post_w, l12t, l3t, out):
    with ExitStack() as ctx:
        def sb(name, shape, dt):
            return ctx.enter_context(nc.sbuf_tensor(name, shape, dt))

        def sem(name):
            return ctx.enter_context(nc.semaphore(name))

        xres = sb("xres", [P, TILES, D], F32)
        xv = sb("xv", [P, D, TILES], F32)
        x2T = sb("x2T", [P, B * L], F32)
        ring = sb("toeplitz_ring", [P, 4, DG, P], F32)
        vq = sb("vq_tables", [P, 2 * TAB], F32)
        ident = sb("ident", [P, P], F32)
        flip = sb("flip", [P, P], F32)
        ones_f = sb("ones_f", [P, P], F32)
        ones_b = sb("ones_b", [P, P], BF16)
        w1 = sb("w1", [P, FF], F16)
        w2 = sb("w2", [P, NF, D], F16)
        b1 = sb("b1", [P, NF], F32)
        brow = sb("brow", [P, MIX_C + D], BF16)
        wk_hi = sb("wk_hi", [P, K, 3 * D], F16)
        wk_lo = sb("wk_lo", [P, K, 3 * D], F16)
        wo = sb("wo", [P, D], F32)
        l12_hi = sb("l12_hi", [P, 2 * NG, GP], F16)
        l12_lo = sb("l12_lo", [P, 2 * NG, GP], F16)
        l3 = sb("l3", [GP, NG, D], F32)
        sbx2 = sb("sbx2", [P, 1], F32)
        prew = sb("prew", [P, 1], F32)
        postw = sb("postw", [P, 1], F32)
        lp = sb("lp", [P, NGR], F32)
        res = sb("res", [P, NGR], F32)
        dsk = sb("dsk", [DG, NGR], F32)
        decay = sb("decay", [P, NGR], F32)
        rp = sb("rp", [P, NGR], F32)
        sel = sb("sel", [P, DG], F32)
        carry = sb("carry", [P, TILES], F32)
        mhalf = sb("mhalf", [P, T4], F32)
        ln_eps = sb("ln_eps", [P, T4], F32)
        rms_eps = sb("rms_eps", [P, T4], F32)
        inv_d = sb("inv_d", [P, T4], F32)
        negm1 = sb("negm1", [P, TILES], F32)
        rstd1 = sb("rstd1", [P, TILES], F32)
        small = sb("small", [P, 8], F32)

        xn = sb("xn", [P, 2, T4, P], F32)
        xnT_hi = sb("xnT_hi", [P, 2, BT], F16)
        xnT_lo = sb("xnT_lo", [P, 2, BT], F16)
        h32 = sb("h32", [P, 2, BT], F32)
        h_hi = sb("h_hi", [P, 2, NF, BT], F16)
        h_lo = sb("h_lo", [P, 2, NF, BT], F16)
        bnst = sb("bnst", [P, 2, T4, 6], F32)
        mv = sb("mv", [P, 2, 6, T4], F32)
        fs = sb("fs", [P, 2, 2, T4], F32)
        xin = sb("xin", [P, 2, T4, P], F32)
        xinT_hi = sb("xinT_hi", [P, 2 + L], F16)
        xinT_lo = sb("xinT_lo", [P, 2 + L], F16)
        bnst2 = sb("bnst2", [P, 2, T4, 6], F32)
        mv2 = sb("mv2", [P, 2, 6, T4], F32)
        ms = sb("ms", [P, 2, 7, T4], F32)
        vt = sb("vt", [P, 2, 2, P], F32)
        qs = sb("qs", [P, 4, P], F32)
        vs = sb("vs", [P, 4, P], F32)
        ssum = sb("ssum", [P, 2, TILES], F32)
        dk = sb("dk", [P, 2, TILES], F32)
        state = sb("state", [P, 2, TILES], F32)
        ss = sb("ss", [P, 2, T4], F32)
        rr = sb("rr", [P, 2, 3, T4], F32)

        setup_a = x2T[:, :]
        w1s, w2s = setup_a[:, 0:512], setup_a[:, 512:1024]
        wins, srows = setup_a[:, 1024:1408], setup_a[:, 1408:2560]
        l12s, brs = setup_a[:, 2560:3232], setup_a[:, 3232:3616]
        pow_t, tmp_a = setup_a[:, 4096:6144], setup_a[:, 6144:8192]
        setup_b = xv[:, :, :].rearrange("p a b -> p (a b)")
        exponents, res_pow = setup_b[:, 0:TAB], setup_b[:, 2 * TAB:3 * TAB]
        ring_flat = ring[:, :, :, :].rearrange("p a b c -> p (a b c)")
        hp = ring_flat[0:DG, 0:NGR * HW].rearrange("p (g w) -> p g w", g=NGR)
        iota_t = h32[:, 0, 0:P]
        q_all, v_all = vq[:, 0:TAB], vq[:, TAB:2 * TAB]
        gm = h_hi[:, :, :, :].rearrange("p a b c -> p (a b c)").bitcast(F32).rearrange(
            "p (a d t) -> p a d t", a=4, d=DG)[:, 0:2]
        masked = h_lo[:, 0, :, :].rearrange("p b c -> p (b c)").bitcast(F32)[:, 0:DG * TILES].rearrange(
            "p (d t) -> p d t", d=DG)
        gg = ring_flat[0:GP, 0:2 * NG * BT].rearrange("p (a f t) -> p a f t", a=2, f=NG)
        yxT = ring_flat[:, 2 * NG * BT:2 * NG * BT + 2 * BT].rearrange("p (a t) -> p a t", a=2)
        u_sb = vq[:, 0:2 * BT].rearrange("p (a t d) -> p a t d", a=2, t=T4)
        y_sb = vq[:, 2 * BT:4 * BT].rearrange("p (a t d) -> p a t d", a=2, t=T4)
        g1 = vq[0:GP, 4 * BT:6 * BT].rearrange("p (a t) -> p a t", a=2)
        yst, zm, zT_hi, zT_lo = xin, xn, xnT_hi, xnT_lo

        bank = [ctx.enter_context(nc.psum_tensor(f"bank{n}", [P, BT], F32)) for n in range(8)]
        ps_xnT, ps_up, ps_down, ps_inT = bank[0], bank[1:3], bank[3], bank[4]
        ps_mix, ps_x2 = bank[5:7], bank[7]
        ps_state, ps_conv = bank[0:2], bank[2:4]
        ps_yT, ps_proj, ps_l1, ps_zT, ps_l2, ps_l3 = bank[0], bank[1], bank[2:4], bank[4], bank[5:7], bank[7]

        hpad = nc.dram_tensor("impulse", [D, HW], F32, kind="Internal")

        ffn_w_loaded, mix_w_loaded, x_loaded = sem("ffn_w_loaded"), sem("mix_w_loaded"), sem("x_loaded")
        impulse_stored, out_stored = sem("impulse_stored"), sem("out_stored")
        toeplitz_loaded = [sem(f"toeplitz_loaded{s}") for s in range(4)]
        cleared = sem("cleared")
        consts, abs_summed, abs_total, dve_step = sem("consts"), sem("abs_summed"), sem("abs_total"), sem("dve_step")
        args_ready, powers, impulse_mm, impulse_ready = (
            sem("args_ready"), sem("powers"), sem("impulse_mm"), sem("impulse_ready"))
        pow_T, tables_ready, weights_ready, sel_ready = (
            sem("pow_T"), sem("tables_ready"), sem("weights_ready"), sem("sel_ready"))
        ternary_ready = sem("ternary_ready")
        ffn_square, mix_square, mix_scale = sem("ffn_square"), sem("mix_square"), sem("mix_scale")
        ffn_bn, ffn_stats, ffn_var, ffn_centred, ffn_normed = (
            sem("ffn_bn"), sem("ffn_stats"), sem("ffn_var"), sem("ffn_centred"), sem("ffn_normed"))
        ffn_T, ffn_hi, ffn_lo, up_done, gelu_done, hid_lo, down_done, resid_done = (
            sem("ffn_T"), sem("ffn_hi"), sem("ffn_lo"), sem("up_done"), sem("gelu_done"), sem("hid_lo"),
            sem("down_done"), sem("resid_done"))
        mix_bn, mix_stats, mix_step, mix_normed, mix_T, mix_hi, mix_lo = (
            sem("mix_bn"), sem("mix_stats"), sem("mix_step"), sem("mix_normed"), sem("mix_T"), sem("mix_hi"),
            sem("mix_lo"))
        mix_mm, v_copied, xv_done, x2_mm, x2_stored = (
            sem("mix_mm"), sem("v_copied"), sem("xv_done"), sem("x2_mm"), sem("x2_stored"))
        tab_ready, state_mm, masked_done, summed, decay_ready, scanned, carry_ready, conv_mm, y_stored = (
            sem("tab_ready"), sem("state_mm"), sem("masked_done"), sem("summed"), sem("decay_ready"),
            sem("scanned"), sem("carry_ready"), sem("conv_mm"), sem("y_stored"))
        y_staged, y_T, gated, proj_mm, u_centred, u_ready, y_sum, squared = (
            sem("y_staged"), sem("y_T"), sem("gated"), sem("proj_mm"), sem("u_centred"), sem("u_ready"),
            sem("y_sum"), sem("squared"))
        z_var, z_rstd, z_ready, xy_done, z_T, z_hi, z_lo = (
            sem("z_var"), sem("z_rstd"), sem("z_ready"), sem("xy_done"), sem("z_T"), sem("z_hi"), sem("z_lo"))
        l12_mm, g1_done, glu_done, l3_mm, mixed = (
            sem("l12_mm"), sem("g1_done"), sem("glu_done"), sem("l3_mm"), sem("mixed"))

        block = ctx.enter_context(nc.Block())

        def tiles_of(t, i):
            return t[:, bass.ds(i * T4, T4), :]

        def per_tile(stat):
            return stat.unsqueeze(2).to_broadcast([P, T4, D])

        @block.sync
        def _(sp):
            sp.dma_start(tiles_of(xres, 0), x[:, 0:T4, :]).then_inc(x_loaded, 16)
            for dst, src in ((w1s, w1t), (w2s, w2t), (b1[:], b1c)):
                sp.dma_start(dst, src).then_inc(ffn_w_loaded, 16)
            for dst, src in ((brs, bias_rows), (prew[:], pre_w), (wins, wint), (srows, short_rows),
                             (sbx2[:], short_bc), (lp[:], poles), (res[:], residues), (dsk[:], dskip),
                             (wo[:], wot), (postw[:], post_w), (l12s, l12t), (l3[:], l3t)):
                sp.dma_start(dst, src).then_inc(mix_w_loaded, 16)
            with sp.Fori(1, NB) as i:
                sp.wait_ge(x_loaded, i * 16)
                sp.dma_start(tiles_of(xres, i), x[:, bass.ds(i * T4, T4), :]).then_inc(x_loaded, 16)
            sp.wait_ge(impulse_ready, 1)
            sp.dma_start(hpad.ap().rearrange("(g p) w -> p g w", p=DG), hp).then_inc(impulse_stored, 16)
            sp.wait_ge(impulse_stored, 16)
            for g in range(NGR):
                after(sp, conv_mm, g - 3)
                src = bass.AP(hpad, g * DG * HW, [[1, P], [HW, DG], [1, P]])
                sp.dma_start(ring[:, g % 4, :, :], src).then_inc(toeplitz_loaded[g % 4], 16)
            with sp.Fori(0, NB) as i:
                sp.wait_ge(resid_done, i + (NB + 1))
                sp.dma_start(out[:, bass.ds(i * T4, T4), :], tiles_of(xres, i)).then_inc(out_stored, 16)
            sp.wait_ge(out_stored, 16 * NB)

        @block.tensor
        def _(pe):
            pe.wait_ge(abs_summed, 1)
            pe.wait_ge(consts, 1)
            pe.matmul(ps_x2[:, 0:2], ones_f[:], small[:, 0:2], start=True, stop=True).then_inc(abs_total, 1)
            pe.wait_ge(powers, 2)
            pe.wait_ge(sel_ready, 2)
            for q in range(4):
                pe.matmul(bank[q][0:DG, :], sel[:], res_pow[:, q * BT:(q + 1) * BT], start=True, stop=True)\
                    .then_inc(impulse_mm, 1)
            for g in range(NGR):
                if g == 3 * 4:
                    pe.wait_ge(ternary_ready, 1)
                last = pe.transpose(bank[4 + g // 4][:, (g % 4) * P:(g % 4 + 1) * P],
                                    pow_t[:, g * P:(g + 1) * P], ident[:])
                if g % 4 == 3:
                    last.then_inc(pow_T, 1)
            pe.wait_ge(weights_ready, 1)
            pe.wait_ge(tables_ready, 7)

            def ffn_transpose(n, par):
                pe.wait_ge(ffn_normed, n + 1)
                after(pe, ffn_lo, n)
                for t in range(T4):
                    last = pe.transpose(ps_xnT[:, t * P:(t + 1) * P], xn[:, par, t, :], ident[:])
                last.then_inc(ffn_T, 1)

            def ffn_up(n, par, f):
                if f == 0:
                    pe.wait_ge(ffn_lo, n + 1)
                after(pe, gelu_done, n * NF + f - 1)
                o = ps_up[f % 2][:]
                pe.matmul(o, w1[:, f * P:(f + 1) * P], xnT_hi[:, par, :], start=True, stop=False)
                pe.matmul(o, w1[:, f * P:(f + 1) * P], xnT_lo[:, par, :], start=False, stop=True)\
                    .then_inc(up_done, 1)

            def ffn_down(n, par):
                pe.wait_ge(hid_lo, n * NF + NF)
                after(pe, resid_done, n)
                for t in range(T4):
                    o = ps_down[:, t * P:(t + 1) * P]
                    pe.matmul(o, ones_b[:], brow[:, MIX_C:MIX_C + D], start=True, stop=False)
                    for f in range(NF):
                        cut = slice(t * P, (t + 1) * P)
                        pe.matmul(o, h_hi[:, par, f, cut], w2[:, f, :], start=False, stop=False)
                        last = pe.matmul(o, h_lo[:, par, f, cut], w2[:, f, :], start=False, stop=f == NF - 1)
                last.then_inc(down_done, 1)

            def mix_transpose(i, par):
                pe.wait_ge(mix_normed, i + 1)
                after(pe, mix_lo, i)
                for t in range(T4):
                    last = pe.transpose(ps_inT[:, t * P:(t + 1) * P], xin[:, par, t, :], ident[:])
                last.then_inc(mix_T, 1)

            def mix_project(j, par, pair):
                if pair == 0:
                    pe.wait_ge(mix_lo, j + 1)
                after(pe, xv_done, j * 2 + (pair - 1))
                for a in range(2):
                    o = ps_mix[pair][:, a * MIX_C:(a + 1) * MIX_C]
                    pe.matmul(o, ones_b[:], brow[:, 0:MIX_C], start=True, stop=False)
                    for k in range(K):
                        at = par * BT + (2 * pair + a) * P + k
                        hi, lo = xinT_hi[:, at:at + P], xinT_lo[:, at:at + P]
                        pe.matmul(o, hi, wk_hi[:, k, D:3 * D], start=False, stop=False)
                        pe.matmul(o, hi, wk_lo[:, k, D:3 * D], start=False, stop=False)
                        last = pe.matmul(o, lo, wk_hi[:, k, D:3 * D], start=False, stop=k == K - 1)
                last.then_inc(mix_mm, 1)

            def mix_project_x2(j, par):
                after(pe, x2_stored, j)
                for k in range(K):
                    at = par * BT + k
                    pe.matmul(ps_x2[:], wk_hi[:, k, 0:D], xinT_hi[:, at:at + BT], start=k == 0, stop=False)
                    pe.matmul(ps_x2[:], wk_hi[:, k, 0:D], xinT_lo[:, at:at + BT], start=False, stop=False)
                    last = pe.matmul(ps_x2[:], wk_lo[:, k, 0:D], xinT_hi[:, at:at + BT], start=False,
                                     stop=k == K - 1)
                last.then_inc(x2_mm, 1)

            ffn_transpose(0, 0)

            def step(i, par, known):
                ffn_up(i, par, 0)
                ffn_up(i, par, 1)
                if known != NB - 1:
                    ffn_transpose(i + 1, 1 - par)
                if known is None or known >= 2:
                    mix_project(i - 2, par, 0)
                ffn_up(i, par, 2)
                if known is None or known >= 2:
                    mix_project(i - 2, par, 1)
                ffn_up(i, par, 3)
                if known is None or known >= 2:
                    mix_project_x2(i - 2, par)
                ffn_down(i, par)
                if known != 0:
                    mix_transpose(i - 1, 1 - par)

            each_block(pe, step, 4)
            mix_transpose(NB - 1, 1)
            for j in (NB - 2, NB - 1):
                mix_project(j, j % 2, 0)
                mix_project(j, j % 2, 1)
                mix_project_x2(j, j % 2)

            pe.wait_ge(xv_done, 2 * NB)
            pe.wait_ge(resid_done, NB)

            def group_rhs(g):
                return xv[:, bass.ds(g * DG, DG), :].rearrange("p a b -> p (a b)")

            def conv_state(g, s):
                pe.wait_ge(tab_ready, g + 1)
                after(pe, masked_done, g - 1)
                pe.matmul(ps_state[s % 2][:], vs[:, s, :], group_rhs(g), start=True, stop=True)\
                    .then_inc(state_mm, 1)

            def conv_from_states(g, s):
                pe.wait_ge(carry_ready, g + 1)
                after(pe, y_stored, g - 1)
                pe.matmul(ps_conv[s % 2][:], qs[:, s, :], gm[:, s % 2, :, :].rearrange("p d t -> p (d t)"),
                          start=True, stop=True, skip_group_check=True)

            def conv_in_chunk(g, s, turn):
                pe.wait_ge(toeplitz_loaded[s], turn * 16 + 16)
                for c in range(DG):
                    last = pe.matmul(ps_conv[s % 2][:, c * TILES:(c + 1) * TILES], ring[:, s, c, :],
                                     xv[:, bass.ds(g * DG + c, 1), :].rearrange("p a b -> p (a b)"),
                                     start=False, stop=True, skip_group_check=True)
                last.then_inc(conv_mm, 1)

            def conv_turn(turn, last_turn=False):
                for s in range(4):
                    conv_from_states(turn * 4 + s, s)
                    if not (last_turn and s >= 2):
                        conv_state(turn * 4 + (s + 2), (s + 2) % 4)
                    conv_in_chunk(turn * 4 + s, s, turn)

            conv_state(0, 0)
            conv_state(1, 1)
            conv_turn(0)
            with pe.Fori(1, NGR // 4 - 1) as turn:
                conv_turn(turn)
            conv_turn(NGR // 4 - 1, True)

            def y_transpose(i, par):
                pe.wait_ge(y_staged, i + 1)
                after(pe, gated, i)
                for t in range(T4):
                    last = pe.transpose(ps_yT[:, t * P:(t + 1) * P], yst[:, par, t, :], flip[:])
                last.then_inc(y_T, 1)

            def project_out(i, par):
                pe.wait_ge(gated, i + 1)
                after(pe, y_sum, i)
                for t in range(T4):
                    last = pe.matmul(ps_proj[:, t * P:(t + 1) * P], yxT[:, par, t * P:(t + 1) * P], wo[:],
                                     start=True, stop=True)
                last.then_inc(proj_mm, 1)

            def z_transpose(i, par):
                pe.wait_ge(z_ready, i + 1)
                after(pe, z_lo, i)
                for t in range(T4):
                    last = pe.transpose(ps_zT[:, t * P:(t + 1) * P], zm[:, par, t, :], ident[:])
                last.then_inc(z_T, 1)

            def gate_up(i, par, f):
                if f == 0:
                    pe.wait_ge(z_lo, i + 1)
                b = (NG * par + f) % 2
                after(pe, glu_done, i * NG + (f - 1))
                for m, ps in ((f, ps_l1[b]), (NG + f, ps_l2[b])):
                    o = ps[0:GP, :]
                    pe.matmul(o, l12_hi[:, m, :], zT_hi[:, par, :], start=True, stop=False)
                    pe.matmul(o, l12_hi[:, m, :], zT_lo[:, par, :], start=False, stop=False)
                    last = pe.matmul(o, l12_lo[:, m, :], zT_hi[:, par, :], start=False, stop=True)
                last.then_inc(l12_mm, 1)

            def gate_down(i, par):
                pe.wait_ge(glu_done, i * NG + NG)
                after(pe, mixed, i)
                for t in range(T4):
                    for f in range(NG):
                        last = pe.matmul(ps_l3[:, t * P:(t + 1) * P], gg[:, par, f, t * P:(t + 1) * P],
                                         l3[:, f, :], start=f == 0, stop=f == NG - 1)
                last.then_inc(l3_mm, 1)

            pe.wait_ge(masked_done, NGR)
            pe.wait_ge(y_stored, NGR)
            for i in range(2):
                y_transpose(i, i)
                project_out(i, i)
            z_transpose(0, 0)

            def step(i, par, known):
                gate_up(i, par, 0)
                if known is None or known < NB - 2:
                    y_transpose(i + 2, par)
                gate_up(i, par, 1)
                if known != NB - 1:
                    z_transpose(i + 1, 1 - par)
                if known != 0:
                    gate_down(i - 1, 1 - par)
                if known is None or known < NB - 2:
                    project_out(i + 2, par)
                gate_up(i, par, 2)

            each_block(pe, step, 2)
            gate_down(NB - 1, 1)

            pe.wait_ge(gated, NB)
            pe.wait_ge(y_sum, NB)
            pe.wait_ge(glu_done, NG * NB)
            ffn_transpose(NB, 0)

            def step(i, par, known):
                ffn_up(i + NB, par, 0)
                ffn_up(i + NB, par, 1)
                if known != 0:
                    ffn_down(i + (NB - 1), 1 - par)
                if known != NB - 1:
                    ffn_transpose(i + (NB + 1), 1 - par)
                ffn_up(i + NB, par, 2)
                ffn_up(i + NB, par, 3)

            each_block(pe, step, 2)
            ffn_down(2 * NB - 1, 1)

        @block.scalar
        def _(act):
            act.wait_ge(ffn_w_loaded, 48)
            act.activation(tmp_a[:, 0:FF], w1s, ACT.Abs, accum_out=small[:, 0:1])
            act.activation(tmp_a[:, FF:2 * FF], w2s, ACT.Abs, accum_out=small[:, 1:2]).then_inc(abs_summed, 1)
            act.wait_ge(args_ready, 1)
            act.activation(pow_t, exponents, ACT.Exp)
            act.activation(decay[:], lp[:], ACT.Exp, scale=float(P)).then_inc(powers, 1)
            for q in range(4):
                act.wait_ge(pow_T, q + 1)
                act.activation(v_all[:, q * BT:(q + 1) * BT], bank[4 + q][:], ACT.Copy).then_inc(tables_ready, 1)

            def ffn_split_hi(n, par):
                act.wait_ge(ffn_T, n + 1)
                act.activation(xnT_hi[:, par, :], ps_xnT[:], ACT.Copy).then_inc(ffn_hi, 1)

            def ffn_gelu(n, par, f):
                act.wait_ge(up_done, n * NF + f + 1)
                after(act, hid_lo, n * NF + f - 1)
                act.activation(h32[:, f % 2, :], ps_up[f % 2][:], ACT.Gelu, bias=b1[:, f:f + 1])
                act.activation(h_hi[:, par, f, :], ps_up[f % 2][:], ACT.Gelu, bias=b1[:, f:f + 1])\
                    .then_inc(gelu_done, 1)

            def mix_split_hi(i, par):
                act.wait_ge(mix_T, i + 1)
                act.activation(xinT_hi[:, 2 + par * BT:2 + (par + 1) * BT], ps_inT[:], ACT.Copy)\
                    .then_inc(mix_hi, 1)

            def copy_v(j, pair):
                act.wait_ge(mix_mm, j * 2 + (pair + 1))
                after(act, xv_done, j * 2 + (pair - 1))
                act.activation(vt[:, pair, :, :], ps_mix[pair][:].rearrange("p (a c) -> p a c", a=2)[:, :, D:2 * D],
                               ACT.Copy).then_inc(v_copied, 1)

            def store_x2(j):
                act.wait_ge(x2_mm, j + 1)
                act.activation(x2T[:, bass.ds(j * BT, BT)], ps_x2[:], ACT.Identity, bias=sbx2[:, 0:1])\
                    .then_inc(x2_stored, 1)

            ffn_split_hi(0, 0)

            def step(i, par, known):
                ffn_gelu(i, par, 0)
                ffn_gelu(i, par, 1)
                if known != NB - 1:
                    ffn_split_hi(i + 1, 1 - par)
                if known is None or known >= 2:
                    copy_v(i - 2, 0)
                ffn_gelu(i, par, 2)
                if known is None or known >= 2:
                    copy_v(i - 2, 1)
                ffn_gelu(i, par, 3)
                if known is None or known >= 2:
                    store_x2(i - 2)
                if known != 0:
                    mix_split_hi(i - 1, 1 - par)

            each_block(act, step, 4)
            mix_split_hi(NB - 1, 1)
            for j in (NB - 2, NB - 1):
                copy_v(j, 0)
                copy_v(j, 1)
                store_x2(j)

            def store_y(g, s):
                act.wait_ge(conv_mm, g + 1)
                act.activation(xv[:, bass.ds(g * DG, DG), :],
                               ps_conv[s % 2][:].rearrange("p (c t) -> p c t", c=DG), ACT.Copy).then_inc(y_stored, 1)

            with act.Fori(0, NGR // 2) as turn:
                for s in range(2):
                    store_y(turn * 2 + s, s)

            def square(i, par):
                act.wait_ge(y_sum, i + 1)
                after(act, z_T, i - 1)
                for t in range(T4):
                    last = act.activation(zm[:, par, t, :], y_sb[:, par, t, :], ACT.Square,
                                          accum_out=ss[:, par, t:t + 1])
                last.then_inc(squared, 1)

            def z_split_hi(i, par):
                act.wait_ge(z_T, i + 1)
                act.activation(zT_hi[:, par, :], ps_zT[:], ACT.Copy).then_inc(z_hi, 1)

            def gate_gelu(i, par, f):
                b = (NG * par + f) % 2
                act.wait_ge(l12_mm, i * NG + (f + 1))
                after(act, glu_done, i * NG + (f - 1))
                act.activation(g1[:, b, :], ps_l1[b][0:GP, :], ACT.Gelu_apprx_tanh).then_inc(g1_done, 1)

            square(0, 0)
            square(1, 1)
            z_split_hi(0, 0)

            def step(i, par, known):
                gate_gelu(i, par, 0)
                gate_gelu(i, par, 1)
                if known != NB - 1:
                    z_split_hi(i + 1, 1 - par)
                if known is None or known < NB - 2:
                    square(i + 2, par)
                gate_gelu(i, par, 2)

            each_block(act, step, 2)

            ffn_split_hi(NB, 0)

            def step(i, par, known):
                ffn_gelu(i + NB, par, 0)
                ffn_gelu(i + NB, par, 1)
                if known != NB - 1:
                    ffn_split_hi(i + (NB + 1), 1 - par)
                ffn_gelu(i + NB, par, 2)
                ffn_gelu(i + NB, par, 3)

            each_block(act, step, 2)

        @block.vector
        def _(dve):
            chain = [0]

            def link(ins):
                chain[0] += 1
                ins.then_inc(dve_step, 1)
                dve.wait_ge(dve_step, chain[0])

            dve.memset(ones_b[:], 1.0)
            dve.memset(ones_f[:], 1.0).then_inc(consts, 1)
            dve.memset(carry[:], 1.0)
            dve.memset(xinT_hi[:, 0:2], 0.0)
            dve.memset(xinT_lo[:, 0:2], 0.0)
            link(dve.memset(hp, 0.0))
            link(dve.memset(carry[:].rearrange("p (b c) -> p b c", b=B)[:, :, 0:1], 0.0))

            dve.wait_ge(abs_total, 1)
            link(dve.tensor_scalar(small[:, 2:4], ps_x2[:, 0:2], 1.0 / (D * FF), 1e-8, ALU.mult, ALU.max))
            dve.tensor_scalar(small[:, 4:6], small[:, 2:4], 0.5, None, ALU.mult)
            link(dve.tensor_scalar(small[:, 6:8], small[:, 2:4], -0.5, None, ALU.mult))
            dve.tensor_scalar(tmp_a[:, 2 * FF:3 * FF], w1s, small[:, 6:7], None, ALU.is_lt)
            link(dve.tensor_scalar(tmp_a[:, 3 * FF:4 * FF], w2s, small[:, 7:8], None, ALU.is_lt))
            dve.scalar_tensor_tensor(w1[:], w1s, small[:, 4:5], tmp_a[:, 2 * FF:3 * FF], ALU.is_gt, ALU.subtract)
            dve.scalar_tensor_tensor(w2[:].rearrange("p f d -> p (f d)"), w2s, small[:, 5:6],
                                     tmp_a[:, 3 * FF:4 * FF], ALU.is_gt, ALU.subtract).then_inc(ternary_ready, 1)

            dve.wait_ge(mix_w_loaded, 12 * 16)
            dve.wait_ge(sel_ready, 2)
            lp_cols = lp[:].unsqueeze(2).to_broadcast([P, NGR, P])
            res_cols = res[:].unsqueeze(2).to_broadcast([P, NGR, P])
            dve.tensor_tensor(exponents.rearrange("p (g t) -> p g t", g=NGR), lp_cols,
                              iota_t.unsqueeze(1).to_broadcast([P, NGR, P]), ALU.mult).then_inc(args_ready, 1)

            wprime, wk = tmp_a[:, 0:3 * D], setup_a[:, 6144 + 512:6144 + 512 + K * 3 * D]
            dve.wait_ge(ternary_ready, 1)
            link(dve.tensor_scalar(wprime, wins, prew[:, 0:1], None, ALU.mult))
            wk3 = wk.rearrange("p (k c) -> p k c", k=K)
            link(dve.tensor_tensor(wk3, wprime.unsqueeze(1).to_broadcast([P, K, 3 * D]),
                                   srows.rearrange("p (k c) -> p k c", k=K), ALU.mult))
            link(dve.tensor_copy(wk_hi[:], wk3))
            dve.tensor_tensor(wk_lo[:], wk3, wk_hi[:], ALU.subtract)
            link(dve.tensor_scalar(l12s, l12s, postw[:, 0:1], None, ALU.mult))
            l12v = l12s.rearrange("p (m c) -> p m c", m=2 * NG)
            link(dve.tensor_copy(l12_hi[:], l12v))
            dve.tensor_tensor(l12_lo[:], l12v, l12_hi[:], ALU.subtract)
            nbr = MIX_C + D
            part, rest = xnT_hi[:, 0, :].bitcast(BF16)[:, 0:nbr], tmp_a[:, 1664:1664 + nbr]
            acc = xn[:, 0, :, :].rearrange("p a b -> p (a b)")
            acc2 = xn[:, 1, :, :].rearrange("p a b -> p (a b)")
            link(dve.tensor_copy(part, brs))
            dve.tensor_tensor(rest, brs, part, ALU.subtract)
            link(dve.tensor_scalar(acc[:, 0:nbr], part, ident[:, 0:1], None, ALU.mult))
            link(dve.tensor_copy(part, rest))
            link(dve.tensor_tensor(rest, rest, part, ALU.subtract))
            link(dve.scalar_tensor_tensor(acc2[:, 0:nbr], part, ident[:, 1:2], acc[:, 0:nbr], ALU.mult, ALU.add))
            link(dve.scalar_tensor_tensor(brow[:], rest, ident[:, 2:3], acc2[:, 0:nbr], ALU.mult, ALU.add))

            dve.wait_ge(powers, 1)
            pow3 = pow_t.rearrange("p (g t) -> p g t", g=NGR)
            dve.tensor_tensor(res_pow.rearrange("p (g t) -> p g t", g=NGR), pow3, res_cols, ALU.mult)\
                .then_inc(powers, 1)
            link(dve.tensor_tensor(rp[:].unsqueeze(2), res[:].unsqueeze(2), pow3[:, :, P - 2:P - 1], ALU.mult))
            dve.tensor_tensor(q_all.rearrange("p (g t) -> p g t", g=NGR), pow3,
                              rp[:].unsqueeze(2).to_broadcast([P, NGR, P]), ALU.mult).then_inc(tables_ready, 1)
            for q in range(4):
                dve.wait_ge(impulse_mm, q + 1)
                link(dve.tensor_copy(hp[:, 4 * q:4 * q + 4, 0:P],
                                     bank[q][0:DG, :].rearrange("p (g t) -> p g t", g=4)))
            dve.tensor_tensor(hp[:, :, P - 1:P], hp[:, :, P - 1:P], dsk[:].unsqueeze(2), ALU.add)\
                .then_inc(impulse_ready, 1)
            dve.wait_ge(impulse_ready, 1)
            dve.tensor_copy(small[:, 0:1], ones_f[:, 0:1]).then_inc(weights_ready, 1)
            dve.tensor_copy(small[:, 1:2], ones_f[:, 0:1]).then_inc(tables_ready, 2)

            def stats(n, par, buf, agg, sems, tile_block):
                half, square, out_sem = sems
                for t in range(T4):
                    last = dve.bn_stats(buf[:, par, t, 0:6], xres[:, bass.ds(tile_block * T4 + t, 1), :]
                                        .rearrange("p a d -> p (a d)"))
                last.then_inc(half, 1)
                b, m = buf[:, par], agg[:, par]
                dve.wait_ge(half, n + 1)
                dve.tensor_tensor(m[:, 2, :], b[:, :, 1], b[:, :, 4], ALU.add)
                dve.tensor_tensor(m[:, 3, :], b[:, :, 1], b[:, :, 4], ALU.subtract)
                dve.tensor_tensor(m[:, 4, :], b[:, :, 2], b[:, :, 5], ALU.add).then_inc(square, 1)
                dve.wait_ge(square, n * 2 + 1)
                dve.tensor_scalar(m[:, 0, :], m[:, 2, :], -0.5, None, ALU.mult)
                dve.scalar_tensor_tensor(m[:, 5, :], m[:, 3, :], 0.25, m[:, 3, :], ALU.mult, ALU.mult)\
                    .then_inc(square, 1)
                dve.wait_ge(square, n * 2 + 2)
                dve.scalar_tensor_tensor(m[:, 1, :], m[:, 4, :], 1.0 / D, m[:, 5, :], ALU.mult, ALU.add)\
                    .then_inc(out_sem, 1)

            def ffn_stat(n, i, par):
                after(dve, ffn_normed, n - 1)
                stats(n, par, bnst, mv, (ffn_bn, ffn_square, ffn_stats), i)

            def ffn_split_lo(n, par):
                dve.wait_ge(ffn_hi, n + 1)
                dve.tensor_tensor(xnT_lo[:, par, :], ps_xnT[:], xnT_hi[:, par, :], ALU.subtract).then_inc(ffn_lo, 1)

            def hidden_lo(n, par, f):
                dve.wait_ge(gelu_done, n * NF + f + 1)
                dve.tensor_tensor(h_lo[:, par, f, :], h32[:, f % 2, :], h_hi[:, par, f, :], ALU.subtract)\
                    .then_inc(hid_lo, 1)

            def ffn_residual(n, i):
                dve.wait_ge(down_done, n + 1)
                xb = tiles_of(xres, i).rearrange("p t d -> p (t d)")
                dve.scalar_tensor_tensor(xb, ps_down[:], 0.5, xb, ALU.mult, ALU.add).then_inc(resid_done, 1)

            def mix_stat(i, par):
                stats(i, par, bnst2, mv2, (mix_bn, mix_square, mix_stats), i)

            def mix_split_lo(i, par):
                dve.wait_ge(mix_hi, i + 1)
                cut = slice(2 + par * BT, 2 + (par + 1) * BT)
                dve.tensor_tensor(xinT_lo[:, cut], ps_inT[:], xinT_hi[:, cut], ALU.subtract).then_inc(mix_lo, 1)

            def gate_x1_v(j, pair):
                dve.wait_ge(v_copied, j * 2 + (pair + 1))
                dve.tensor_tensor(xv[:, :, bass.ds(j * T4 + 2 * pair, 2)],
                                  ps_mix[pair][:].rearrange("p (a c) -> p c a", a=2)[:, 0:D, :],
                                  vt[:, pair, :, :].rearrange("p a c -> p c a"), ALU.mult).then_inc(xv_done, 1)

            for i in range(2):
                dve.wait_ge(x_loaded, 16 * (i + 1))
                ffn_stat(i, i, i)
            ffn_split_lo(0, 0)

            def step(i, par, known):
                if known is None or known < NB - 2:
                    dve.wait_ge(x_loaded, i * 16 + 48)
                    ffn_stat(i + 2, i + 2, par)
                hidden_lo(i, par, 0)
                hidden_lo(i, par, 1)
                if known != NB - 1:
                    ffn_split_lo(i + 1, 1 - par)
                if known is None or known >= 2:
                    gate_x1_v(i - 2, 0)
                hidden_lo(i, par, 2)
                if known is None or known >= 2:
                    gate_x1_v(i - 2, 1)
                hidden_lo(i, par, 3)
                ffn_residual(i, i)
                dve.wait_ge(resid_done, i + 1)
                after(dve, mix_normed, i - 1)
                if known != 0:
                    mix_split_lo(i - 1, 1 - par)
                mix_stat(i, par)

            each_block(dve, step, 4)
            mix_split_lo(NB - 1, 1)
            for j in (NB - 2, NB - 1):
                gate_x1_v(j, 0)
                gate_x1_v(j, 1)

            mask_cols = sel[:].unsqueeze(2).to_broadcast([P, DG, TILES])
            dve.wait_ge(hid_lo, NF * NB)
            dve.wait_ge(down_done, NB)
            dve.memset(gm, 0.0).then_inc(dve_step, 1)
            chain[0] += 1
            dve.wait_ge(dve_step, chain[0])

            def carry_states(g, s):
                par = s % 2
                dve.tensor_scalar(dk[:, par, :], carry[:], decay[:, bass.ds(g, 1)], None, ALU.mult)\
                    .then_inc(decay_ready, 1)
                dve.wait_ge(state_mm, g + 1)
                dve.tensor_tensor(masked, ps_state[par][:].rearrange("p (c t) -> p c t", c=DG), mask_cols, ALU.mult)\
                    .then_inc(masked_done, 1)
                dve.wait_ge(masked_done, g + 1)
                dve.tensor_reduce(ssum[:, par, :], masked.rearrange("p c t -> p t c"), AX_X, ALU.add)\
                    .then_inc(summed, 1)
                dve.wait_ge(summed, g + 1)
                dve.wait_ge(decay_ready, g + 1)
                dve.tensor_tensor_scan(state[:, par, :], dk[:, par, :], ssum[:, par, :], 0.0, ALU.mult, ALU.add)\
                    .then_inc(scanned, 1)
                dve.wait_ge(scanned, g + 1)
                after(dve, conv_mm, g - 1)
                before = state[:, par, :].rearrange("p (b c) -> p b c", b=B)[:, :, 0:CH - 1]
                into = gm[:, par, :, :].rearrange("p d (b c) -> p d b c", b=B)[:, :, :, 1:CH]
                dve.tensor_tensor(into, before.unsqueeze(1).to_broadcast([P, DG, B, CH - 1]),
                                  sel[:].unsqueeze(2).unsqueeze(3).to_broadcast([P, DG, B, CH - 1]), ALU.mult)\
                    .then_inc(carry_ready, 1)

            for g in range(2):
                carry_states(g, g)
            with dve.Fori(1, NGR // 2) as turn:
                for s in range(2):
                    carry_states(turn * 2 + s, s)

            def stage_y(i, par):
                after(dve, y_T, i - 1)
                dve.tensor_copy(yst[:, par, :, :], xv[:, :, bass.ds(i * T4, T4)].rearrange("p d t -> p t d"))\
                    .then_inc(y_staged, 1)

            def gate_y(i, par):
                dve.wait_ge(y_T, i + 1)
                after(dve, proj_mm, i - 1)
                dve.tensor_tensor(yxT[:, par, :], ps_yT[:], x2T[:, bass.ds(i * BT, BT)], ALU.mult)\
                    .then_inc(gated, 1)

            def sum_y(i, par):
                dve.wait_ge(proj_mm, i + 1)
                dve.wait_ge(u_ready, i + 1)
                after(dve, xy_done, i - 1)
                dve.tensor_tensor(y_sb[:, par, :, :], ps_proj[:].rearrange("p (t d) -> p t d", t=T4),
                                  u_sb[:, par, :, :], ALU.add).then_inc(y_sum, 1)

            def z_split_lo(i, par):
                dve.wait_ge(z_hi, i + 1)
                dve.tensor_tensor(zT_lo[:, par, :], ps_zT[:], zT_hi[:, par, :], ALU.subtract).then_inc(z_lo, 1)

            def glu(i, par, f):
                b = (NG * par + f) % 2
                dve.wait_ge(g1_done, i * NG + (f + 1))
                if f == 0:
                    after(dve, l3_mm, i - 1)
                dve.tensor_tensor(gg[:, par, f, :], ps_l2[b][0:GP, :], g1[:, b, :], ALU.mult).then_inc(glu_done, 1)

            def mixer_residual(i):
                dve.wait_ge(l3_mm, i + 1)
                dve.wait_ge(xy_done, i + 1)
                xb = tiles_of(xres, i).rearrange("p t d -> p (t d)")
                dve.tensor_tensor(xb, ps_l3[:], xb, ALU.add).then_inc(mixed, 1)

            dve.wait_ge(y_stored, NGR)
            stage_y(0, 0)
            stage_y(1, 1)
            for i in range(2):
                gate_y(i, i)
                sum_y(i, i)
            stage_y(2, 0)
            z_split_lo(0, 0)

            def step(i, par, known):
                if known is None or known < NB - 3:
                    stage_y(i + 3, 1 - par)
                glu(i, par, 0)
                if known is None or known < NB - 2:
                    gate_y(i + 2, par)
                glu(i, par, 1)
                if known != NB - 1:
                    z_split_lo(i + 1, 1 - par)
                if known != 0:
                    mixer_residual(i - 1)
                if known is None or known < NB - 2:
                    sum_y(i + 2, par)
                glu(i, par, 2)

            each_block(dve, step, 2, 4)
            mixer_residual(NB - 1)

            dve.wait_ge(mixed, NB)
            ffn_stat(NB, 0, 0)
            ffn_stat(NB + 1, 1, 1)
            ffn_split_lo(NB, 0)

            def step(i, par, known):
                if known is None or known < NB - 2:
                    ffn_stat(i + (NB + 2), i + 2, par)
                hidden_lo(i + NB, par, 0)
                hidden_lo(i + NB, par, 1)
                if known != 0:
                    ffn_residual(i + (NB - 1), i - 1)
                if known != NB - 1:
                    ffn_split_lo(i + (NB + 1), 1 - par)
                hidden_lo(i + NB, par, 2)
                hidden_lo(i + NB, par, 3)

            each_block(dve, step, 2)
            ffn_residual(2 * NB - 1, NB - 1)

        @block.gpsimd
        def _(pool):
            pool.memset(mhalf[:], -0.5)
            pool.memset(ln_eps[:], LN_EPS)
            pool.memset(rms_eps[:], RMS_EPS)
            pool.memset(inv_d[:], 1.0 / D)
            pool.memset(sel[:], 1.0)
            pool.memset(flip[:], 0.0)
            pool.memset(ident[:], 0.0).then_inc(cleared, 1)
            pool.wait_ge(cleared, 1)
            pool.affine_select(ident[:], ident[:], pattern=[[-1, P]], compare_op=ALU.not_equal, fill=1.0,
                               base=0, channel_multiplier=1)
            pool.affine_select(flip[:], flip[:], pattern=[[1, P]], compare_op=ALU.not_equal, fill=1.0,
                               base=1 - P, channel_multiplier=1)
            pool.iota(iota_t, pattern=[[-1, P]], base=P - 1, channel_multiplier=0, allow_small_or_imprecise_dtypes=True)
            pool.affine_select(sel[:], sel[:], pattern=[[-S, DG]], compare_op=ALU.is_ge, fill=0.0,
                               base=0, channel_multiplier=1).then_inc(sel_ready, 1)
            pool.wait_ge(sel_ready, 1)
            pool.affine_select(sel[:], sel[:], pattern=[[S, DG]], compare_op=ALU.is_ge, fill=0.0,
                               base=S - 1, channel_multiplier=-1).then_inc(sel_ready, 1)

            def ffn_norm(n, i, par):
                pool.wait_ge(ffn_stats, n + 1)
                pool.tensor_tensor(fs[:, par, 0, :], mv[:, par, 1, :], ln_eps[:], ALU.add).then_inc(ffn_var, 1)
                pool.wait_ge(ffn_var, n + 1)
                after(pool, ffn_T, n - 1)
                pool.tensor_tensor(fs[:, par, 1, :], fs[:, par, 0, :], mhalf[:], ALU.pow)
                pool.tensor_tensor(xn[:, par, :, :], tiles_of(xres, i), per_tile(mv[:, par, 0, :]), ALU.add)\
                    .then_inc(ffn_centred, 1)
                pool.wait_ge(ffn_centred, n + 1)
                pool.tensor_tensor(xn[:, par, :, :], xn[:, par, :, :], per_tile(fs[:, par, 1, :]), ALU.mult)\
                    .then_inc(ffn_normed, 1)

            steps = 6

            def mix_norm(i, par):
                cols = bass.ds(i * T4, T4)
                m, negm, var = ms[:, par], mv2[:, par, 0, :], mv2[:, par, 1, :]
                pool.wait_ge(mix_stats, i + 1)
                after(pool, mix_T, i - 1)
                pool.tensor_tensor(m[:, 0, :], var, ln_eps[:], ALU.add).then_inc(mix_step, 1)
                pool.wait_ge(mix_step, i * steps + 1)
                pool.tensor_tensor(m[:, 1, :], m[:, 0, :], mhalf[:], ALU.pow).then_inc(mix_step, 1)
                pool.wait_ge(mix_step, i * steps + 2)
                pool.tensor_tensor(m[:, 2, :], m[:, 1, :], m[:, 1, :], ALU.mult).then_inc(mix_step, 1)
                pool.wait_ge(mix_step, i * steps + 3)
                pool.tensor_tensor(m[:, 3, :], m[:, 2, :], var, ALU.mult).then_inc(mix_step, 1)
                pool.wait_ge(mix_step, i * steps + 4)
                pool.tensor_tensor(m[:, 4, :], m[:, 3, :], rms_eps[:], ALU.add).then_inc(mix_step, 1)
                pool.wait_ge(mix_step, i * steps + 5)
                pool.tensor_tensor(m[:, 5, :], m[:, 4, :], mhalf[:], ALU.pow)
                pool.tensor_tensor(xin[:, par, :, :], tiles_of(xres, i), per_tile(negm), ALU.add)
                pool.tensor_copy(negm1[:, cols], negm)
                pool.tensor_copy(rstd1[:, cols], m[:, 1, :]).then_inc(mix_step, 1)
                pool.wait_ge(mix_step, i * steps + 6)
                pool.tensor_tensor(m[:, 6, :], m[:, 5, :], m[:, 1, :], ALU.mult).then_inc(mix_scale, 1)
                pool.wait_ge(mix_scale, i + 1)
                pool.tensor_tensor(xin[:, par, :, :], xin[:, par, :, :], per_tile(m[:, 6, :]), ALU.mult)\
                    .then_inc(mix_normed, 1)

            pool.wait_ge(weights_ready, 1)
            ffn_norm(0, 0, 0)
            ffn_norm(1, 1, 1)

            def step(i, par, known):
                if known is None or known < NB - 2:
                    ffn_norm(i + 2, i + 2, par)
                mix_norm(i, par)

            each_block(pool, step, 2)

            def stage_tables(g, s):
                after(pool, conv_mm, g - 3)
                pool.tensor_copy(vs[:, s, :], v_all[:, bass.ds(g * P, P)])
                pool.tensor_copy(qs[:, s, :], q_all[:, bass.ds(g * P, P)]).then_inc(tab_ready, 1)

            for g in range(4):
                stage_tables(g, g)
            with pool.Fori(1, NGR // 4) as turn:
                for s in range(4):
                    stage_tables(turn * 4 + s, s)

            def make_u(i, par):
                cols = bass.ds(i * T4, T4)
                after(pool, y_sum, i - 1)
                pool.tensor_tensor(u_sb[:, par, :, :], tiles_of(xres, i), per_tile(negm1[:, cols]), ALU.add)\
                    .then_inc(u_centred, 1)
                pool.wait_ge(u_centred, i + 1)
                pool.tensor_tensor(u_sb[:, par, :, :], u_sb[:, par, :, :], per_tile(rstd1[:, cols]), ALU.mult)\
                    .then_inc(u_ready, 1)

            def z_norm(i, par):
                pool.wait_ge(squared, i + 1)
                pool.tensor_tensor(rr[:, par, 0, :], ss[:, par, :], inv_d[:], ALU.mult).then_inc(z_var, 1)
                pool.wait_ge(z_var, i * 2 + 1)
                pool.tensor_tensor(rr[:, par, 1, :], rr[:, par, 0, :], rms_eps[:], ALU.add).then_inc(z_var, 1)
                pool.wait_ge(z_var, i * 2 + 2)
                pool.tensor_tensor(rr[:, par, 2, :], rr[:, par, 1, :], mhalf[:], ALU.pow).then_inc(z_rstd, 1)
                pool.wait_ge(z_rstd, i + 1)
                pool.tensor_tensor(zm[:, par, :, :], y_sb[:, par, :, :], per_tile(rr[:, par, 2, :]), ALU.mult)\
                    .then_inc(z_ready, 1)
                pool.tensor_tensor(tiles_of(xres, i), tiles_of(xres, i), y_sb[:, par, :, :], ALU.add)\
                    .then_inc(xy_done, 1)

            pool.wait_ge(tab_ready, NGR)
            make_u(0, 0)
            make_u(1, 1)
            z_norm(0, 0)
            z_norm(1, 1)
            make_u(2, 0)

            def step(i, par, known):
                if known is None or known < NB - 2:
                    z_norm(i + 2, par)
                if known is None or known < NB - 3:
                    make_u(i + 3, 1 - par)

            each_block(pool, step, 2, 4)

            pool.wait_ge(z_T, NB)
            ffn_norm(NB, 0, 0)
            ffn_norm(NB + 1, 1, 1)

            def step(i, par, known):
                if known is None or known < NB - 2:
                    ffn_norm(i + (NB + 2), i + 2, par)

            each_block(pool, step, 2)


def kernel(**inputs):
    import numpy as np
    import concourse.bacc as _bacc
    from concourse.bass_utils import run_bass_kernel_spmd as _run

    def arr(name):
        return np.asarray(inputs["L0_" + name])

    def rows(a):
        return np.broadcast_to(a.reshape(1, -1), (P, a.size))

    short = arr("attn_short_w").reshape(3 * D, K)
    short_b, b2 = arr("attn_short_b"), arr("ffn_b2")
    l12 = np.concatenate([arr("attn_l1_w"), arr("attn_l2_w")], axis=0)
    data = {
        "x": arr("attn_u").reshape(TILES, P, D).transpose(1, 0, 2),
        "w1t": arr("ffn_W1").T,
        "b1c": arr("ffn_b1").reshape(NF, P).T,
        "w2t": arr("ffn_W2").T.reshape(NF, P, D).transpose(1, 0, 2).reshape(P, NF * D),
        "bias_rows": rows(np.concatenate([short_b[D:], b2])),
        "pre_w": arr("attn_pre_norm_w").reshape(P, 1),
        "wint": arr("attn_in_proj_w").T,
        "short_rows": rows(short.T),
        "short_bc": short_b[:D].reshape(P, 1),
        "poles": arr("attn_log_poles").reshape(NGR, P).T,
        "residues": arr("attn_residues").reshape(NGR, P).T,
        "dskip": arr("attn_D_skip").reshape(NGR, DG).T,
        "wot": arr("attn_out_proj_w").T,
        "post_w": arr("attn_post_norm_w").reshape(P, 1),
        "l12t": l12.T,
        "l3t": arr("attn_l3_w").T.reshape(NG, GP, D).transpose(1, 0, 2),
    }
    nc = _bacc.Bacc("TRN2", target_bir_lowering=False, num_devices=1)
    arrays, args = {}, []
    for name, a in data.items():
        arrays[name] = np.ascontiguousarray(a)
        args.append(nc.dram_tensor(name, a.shape, F32, kind="ExternalInput").ap())
    args.append(nc.dram_tensor("out", (P, TILES, D), F32, kind="ExternalOutput").ap())
    macaron_kernel(nc, *args)
    r = _run(nc, [arrays], core_ids=[0])
    got = np.asarray(r.results[0]["out"])
    return np.ascontiguousarray(got.transpose(1, 0, 2)).reshape(B, L, D)
```

```python
from contextlib import ExitStack

import concourse.bass as bass
from concourse import mybir

F32 = mybir.dt.float32
F16 = mybir.dt.float16
BF16 = mybir.dt.bfloat16
ALU = mybir.AluOpType
ACT = mybir.ActivationFunctionType
AX_X = mybir.AxisListType.X

P = 128
B, L, D = 8, 1024, 128
FF = 512
NF = FF // P
S = 16
K = 3
GF = 336
GP = 112
NG = GF // GP
TILES = B * L // P
CH = L // P
T4 = 4
BT = T4 * P
NB = TILES // T4
DG = P // S
NGR = D // DG
TAB = NGR * P
HW = 2 * P
LN_EPS = 1e-5
RMS_EPS = 1e-6
MIX_C = 2 * D


def after(eng, sem, count):
    if not (isinstance(count, int) and count <= 0):
        eng.wait_ge(sem, count)


def each_block(eng, step, peel_front, peel_back=2):
    for i in range(peel_front):
        step(i, i % 2, i)
    with eng.Fori(peel_front // 2, (NB - peel_back) // 2) as pair:
        step(pair * 2, 0, None)
        step(pair * 2 + 1, 1, None)
    for i in range(NB - peel_back, NB):
        step(i, i % 2, i)


def macaron_kernel(nc, x, w1t, b1c, w2t, bias_rows, pre_w, wint, short_rows, short_x2, short_bc, poles, residues,
                   dskip, wot, post_w, l12t, l3t, out):
    with ExitStack() as ctx:
        def sb(name, shape, dt):
            return ctx.enter_context(nc.sbuf_tensor(name, shape, dt))

        def sem(name):
            return ctx.enter_context(nc.semaphore(name))

        xres = sb("xres", [P, TILES, D], F32)
        xv = sb("xv", [P, D, TILES], F32)
        x2T = sb("x2T", [P, B * L], F32)
        ring = sb("toeplitz_ring", [P, 4, DG, P], F32)
        vq = sb("vq_tables", [P, 2 * TAB], F32)
        ident = sb("ident", [P, P], F32)
        flip = sb("flip", [P, P], F32)
        ones_f = sb("ones_f", [P, P], F32)
        ones_b = sb("ones_b", [P, P], BF16)
        w1 = sb("w1", [P, FF], F16)
        w2 = sb("w2", [P, NF, D], F16)
        w2_last = sb("w2_last", [P, D], F32)
        b1 = sb("b1", [P, NF], F32)
        brow = sb("brow", [P, MIX_C + D], BF16)
        wk_hi = sb("wk_hi", [P, K, MIX_C], F16)
        wk_lo = sb("wk_lo", [P, K, MIX_C], F16)
        wx2_hi = sb("wx2_hi", [P, D], F16)
        wx2_lo = sb("wx2_lo", [P, D], F16)
        tap_x2 = sb("tap_x2", [P, K], F32)
        wo = sb("wo", [P, D], F32)
        l12_hi = sb("l12_hi", [P, 2 * NG, GP], F16)
        l12_lo = sb("l12_lo", [P, 2 * NG, GP], F16)
        l3 = sb("l3", [GP, NG, D], F32)
        sbx2 = sb("sbx2", [P, 1], F32)
        prew = sb("prew", [P, 1], F32)
        postw = sb("postw", [P, 1], F32)
        lp = sb("lp", [P, NGR], F32)
        res = sb("res", [P, NGR], F32)
        dsk = sb("dsk", [DG, NGR], F32)
        decay = sb("decay", [P, NGR], F32)
        rp = sb("rp", [P, NGR], F32)
        sel_res = sb("sel_res", [P, NGR, DG], F32)
        sel_rp = sb("sel_rp", [P, NGR, DG], F32)
        sel = sb("sel", [P, DG], F32)
        carry = sb("carry", [P, TILES], F32)
        mhalf = sb("mhalf", [P, 2, T4], F32)
        rms_eps = sb("rms_eps", [P, T4], F32)
        inv_d = sb("inv_d", [P, T4], F32)
        negm1 = sb("negm1", [P, TILES], F32)
        rstd1 = sb("rstd1", [P, TILES], F32)
        small = sb("small", [P, 8], F32)

        xn = sb("xn", [P, 2, T4, P], F32)
        xnT_hi = sb("xnT_hi", [P, 2, BT], F16)
        xnT_lo = sb("xnT_lo", [P, 2, BT], F16)
        h32 = sb("h32", [P, NF, BT], F32)
        h_hi = sb("h_hi", [P, 2, NF, BT], F16)
        h_lo = sb("h_lo", [P, 2, NF, BT], F16)
        bnst = sb("bnst", [P, 2, T4, 6], F32)
        mv = sb("mv", [P, 2, 6, T4], F32)
        fs = sb("fs", [P, 2, T4], F32)
        xin = sb("xin", [P, 2, T4, P], F32)
        xinT_hi = sb("xinT_hi", [P, 2 + L], F16)
        xinT_lo = sb("xinT_lo", [P, 2 + L], F16)
        bnst2 = sb("bnst2", [P, 2, T4, 6], F32)
        mv2 = sb("mv2", [P, 2, 8, T4], F32)
        ms = sb("ms", [P, 2, 2, T4], F32)
        x2_raw = sb("x2_raw", [P, 2 + L], F32)
        vt = sb("vt", [P, 2, 2, P], F32)
        qs = sb("qs", [P, 4, P], F32)
        vs = sb("vs", [P, 4, P], F32)
        ssum = sb("ssum", [P, 2, TILES], F32)
        dk = sb("dk", [P, 2, TILES], F32)
        state = sb("state", [P, 2, TILES], F32)
        ss = sb("ss", [P, 2, T4], F32)
        rr = sb("rr", [P, 2, 3, T4], F32)

        setup_a = x2T[:, :]
        w1s, w2s = setup_a[:, 0:512], setup_a[:, 512:1024]
        wins, srows = setup_a[:, 1024:1408], setup_a[:, 1408:1408 + K * MIX_C]
        l12s, brs = setup_a[:, 2560:3232], setup_a[:, 3232:3616]
        tmp_a, iota_t = setup_a[:, 6144:8192], setup_a[:, 4096:4096 + P]
        ring_flat = ring[:, :, :, :].rearrange("p a b c -> p (a b c)")
        hp = ring_flat[0:DG, 0:TAB]
        zeros = ring_flat[:, TAB:TAB + HW - P]
        pow_t, v_all = vq[:, 0:TAB], vq[:, TAB:2 * TAB]
        gm = h_hi[:, :, :, :].rearrange("p a b c -> p (a b c)").bitcast(F32).rearrange(
            "p (a d t) -> p a d t", a=4, d=DG)[:, 0:2]
        masked = h_lo[:, 0, :, :].rearrange("p b c -> p (b c)").bitcast(F32)[:, 0:DG * TILES].rearrange(
            "p (d t) -> p d t", d=DG)
        gg = ring_flat[0:GP, 0:2 * NG * BT].rearrange("p (a f t) -> p a f t", a=2, f=NG)
        yxT = ring_flat[:, 2 * NG * BT:2 * NG * BT + 2 * BT].rearrange("p (a t) -> p a t", a=2)
        u_sb = vq[:, 0:2 * BT].rearrange("p (a t d) -> p a t d", a=2, t=T4)
        y_sb = vq[:, 2 * BT:4 * BT].rearrange("p (a t d) -> p a t d", a=2, t=T4)
        g1 = vq[0:GP, 4 * BT:6 * BT].rearrange("p (a t) -> p a t", a=2)
        yst, zm, zT_hi, zT_lo = xin, xn, xnT_hi, xnT_lo

        h_last = x2T[:, 0:2 * BT].rearrange("p (a t) -> p a t", a=2)

        bank = [ctx.enter_context(nc.psum_tensor(f"bank{n}", [P, BT], F32)) for n in range(8)]
        ps_xnT, ps_up, ps_down, ps_inT = bank[0], bank[1:3], bank[3], bank[4]
        ps_mix, ps_x2 = bank[5:7], bank[7]
        ps_state, ps_conv = bank[0:2], bank[2:4]
        ps_yT, ps_proj, ps_l1, ps_zT, ps_l2, ps_l3 = bank[0], bank[1], bank[2:4], bank[4], bank[5:7], bank[7]
        ps_up2 = bank[1:3] + bank[5:7]

        hpad = nc.dram_tensor("impulse", [D, HW], F32, kind="Internal")

        ffn_w_loaded, small_w_loaded, mix_w_loaded, x_loaded = (
            sem("ffn_w_loaded"), sem("small_w_loaded"), sem("mix_w_loaded"), sem("x_loaded"))
        impulse_stored, out_stored = sem("impulse_stored"), sem("out_stored")
        toeplitz_loaded = [sem(f"toeplitz_loaded{s}") for s in range(4)]
        cleared, consts, sel_ready, zeros_ready = (
            sem("cleared"), sem("consts"), sem("sel_ready"), sem("zeros_ready"))
        abs_summed, abs_total, dve_step = sem("abs_summed"), sem("abs_total"), sem("dve_step")
        w1_ready, w2_ready, bias_ready, weights_ready = (
            sem("w1_ready"), sem("w2_ready"), sem("bias_ready"), sem("weights_ready"))
        powers, sel_res_ready, impulse_mm, impulse_copied, impulse_ready, pow_T, v_ready = (
            sem("powers"), sem("sel_res_ready"), sem("impulse_mm"), sem("impulse_copied"), sem("impulse_ready"),
            sem("pow_T"), sem("v_ready"))
        ffn_square, mix_square = sem("ffn_square"), sem("mix_square")
        ffn_bn, ffn_stats, ffn_centred, ffn_normed = (
            sem("ffn_bn"), sem("ffn_stats"), sem("ffn_centred"), sem("ffn_normed"))
        ffn_T, ffn_hi, ffn_lo, up_done, gelu_done, hid_lo, down_done, resid_done = (
            sem("ffn_T"), sem("ffn_hi"), sem("ffn_lo"), sem("up_done"), sem("gelu_done"), sem("hid_lo"),
            sem("down_done"), sem("resid_done"))
        hid0_lo = sem("hid0_lo")
        hid_lo2 = sem("hid_lo2")
        w2_last_ready = sem("w2_last_ready")
        mix_bn, mix_stats, mix_step, mix_normed, mix_T, mix_hi, mix_lo = (
            sem("mix_bn"), sem("mix_stats"), sem("mix_step"), sem("mix_normed"), sem("mix_T"), sem("mix_hi"),
            sem("mix_lo"))
        mix_mm, v_copied, xv_done, x2_mm, x2_stored, x2_tap, x2_done = (
            sem("mix_mm"), sem("v_copied"), sem("xv_done"), sem("x2_mm"), sem("x2_stored"), sem("x2_tap"),
            sem("x2_done"))
        tab_ready, state_mm, masked_done, summed, decay_ready, scanned, carry_ready, conv_mm, y_stored = (
            sem("tab_ready"), sem("state_mm"), sem("masked_done"), sem("summed"), sem("decay_ready"),
            sem("scanned"), sem("carry_ready"), sem("conv_mm"), sem("y_stored"))
        y_staged, y_T, gated, proj_mm, u_centred, u_ready, y_sum, squared = (
            sem("y_staged"), sem("y_T"), sem("gated"), sem("proj_mm"), sem("u_centred"), sem("u_ready"),
            sem("y_sum"), sem("squared"))
        z_var, z_rstd, z_ready, xy_done, z_T, z_hi, z_lo = (
            sem("z_var"), sem("z_rstd"), sem("z_ready"), sem("xy_done"), sem("z_T"), sem("z_hi"), sem("z_lo"))
        l12_mm, g1_done, glu_done, l3_mm, mixed = (
            sem("l12_mm"), sem("g1_done"), sem("glu_done"), sem("l3_mm"), sem("mixed"))

        block = ctx.enter_context(nc.Block())

        def tiles_of(t, i):
            return t[:, bass.ds(i * T4, T4), :]

        def per_tile(stat):
            return stat.unsqueeze(2).to_broadcast([P, T4, D])

        @block.sync
        def _(sp):
            sp.dma_start(tiles_of(xres, 0), x[:, 0:T4, :]).then_inc(x_loaded, 16)
            for dst, src in ((w1s, w1t), (w2s, w2t), (b1[:], b1c)):
                sp.dma_start(dst, src).then_inc(ffn_w_loaded, 16)
            sp.wait_ge(x_loaded, 16)
            sp.dma_start(tiles_of(xres, 1), x[:, T4:2 * T4, :]).then_inc(x_loaded, 16)
            for dst, src in ((lp[:], poles), (res[:], residues), (dsk[:], dskip), (brs, bias_rows)):
                sp.dma_start(dst, src).then_inc(small_w_loaded, 16)
            for dst, src in ((prew[:], pre_w), (wins, wint), (srows, short_rows), (tap_x2[:], short_x2),
                             (sbx2[:], short_bc), (wo[:], wot), (postw[:], post_w), (l12s, l12t), (l3[:], l3t)):
                sp.dma_start(dst, src).then_inc(mix_w_loaded, 16)
            with sp.Fori(2, NB) as i:
                sp.wait_ge(x_loaded, i * 16)
                sp.dma_start(tiles_of(xres, i), x[:, bass.ds(i * T4, T4), :]).then_inc(x_loaded, 16)
            sp.wait_ge(zeros_ready, 1)
            sp.dma_start(hpad[:, P:HW], zeros).then_inc(impulse_stored, 16)
            sp.wait_ge(impulse_ready, 1)
            sp.dma_start(hpad[:, 0:P].rearrange("(g p) w -> p g w", p=DG),
                         hp.rearrange("p (g w) -> p g w", g=NGR)).then_inc(impulse_stored, 16)
            sp.wait_ge(impulse_stored, 32)
            for g in range(NGR):
                after(sp, conv_mm, g - 3)
                src = bass.AP(hpad, g * DG * HW, [[1, P], [HW, DG], [1, P]])
                sp.dma_start(ring[:, g % 4, :, :], src).then_inc(toeplitz_loaded[g % 4], 16)
            with sp.Fori(0, NB) as i:
                sp.wait_ge(resid_done, i + (NB + 1))
                sp.dma_start(out[:, bass.ds(i * T4, T4), :], tiles_of(xres, i)).then_inc(out_stored, 16)
            sp.wait_ge(out_stored, 16 * NB)

        @block.tensor
        def _(pe):
            pe.wait_ge(abs_summed, 1)
            pe.wait_ge(consts, 1)
            pe.matmul(ps_x2[:, 0:2], ones_f[:], small[:, 0:2], start=True, stop=True).then_inc(abs_total, 1)
            pe.wait_ge(sel_ready, 2)

            def impulse_responses():
                pe.wait_ge(powers, 1)
                pe.wait_ge(sel_res_ready, 1)
                for g in range(NGR):
                    last = pe.matmul(bank[4 + g // 4][0:DG, (g % 4) * P:(g % 4 + 1) * P], sel_res[:, g, :],
                                     pow_t[:, g * P:(g + 1) * P], start=True, stop=True)
                    if g % 4 == 3:
                        last.then_inc(impulse_mm, 1)

            def transpose_powers():
                for g in range(NGR):
                    if g % 4 == 0:
                        pe.wait_ge(impulse_copied, g // 4 + 1)
                    last = pe.transpose(bank[4 + g // 4][:, (g % 4) * P:(g % 4 + 1) * P],
                                        pow_t[:, g * P:(g + 1) * P], ident[:])
                    if g % 4 == 3:
                        last.then_inc(pow_T, 1)

            def ffn_transpose(n, par):
                pe.wait_ge(ffn_normed, n + 1)
                after(pe, ffn_lo, n)
                for t in range(T4):
                    last = pe.transpose(ps_xnT[:, t * P:(t + 1) * P], xn[:, par, t, :], ident[:])
                last.then_inc(ffn_T, 1)

            def ffn_up(n, par, f):
                if f == 0:
                    pe.wait_ge(ffn_lo, n + 1)
                after(pe, gelu_done, n * NF + f - 1)
                o = ps_up[f % 2][:]
                pe.matmul(o, w1[:, f * P:(f + 1) * P], xnT_hi[:, par, :], start=True, stop=False)
                pe.matmul(o, w1[:, f * P:(f + 1) * P], xnT_lo[:, par, :], start=False, stop=True)\
                    .then_inc(up_done, 1)

            def ffn_down(n, par):
                pe.wait_ge(hid_lo, n * (NF - 1) + (NF - 1))
                pe.wait_ge(hid0_lo, n + 1)
                after(pe, resid_done, n)
                for t in range(T4):
                    o = ps_down[:, t * P:(t + 1) * P]
                    pe.matmul(o, ones_b[:], brow[:, MIX_C:MIX_C + D], start=True, stop=False)
                    for f in range(NF):
                        cut = slice(t * P, (t + 1) * P)
                        pe.matmul(o, h_hi[:, par, f, cut], w2[:, f, :], start=False, stop=False)
                        last = pe.matmul(o, h_lo[:, par, f, cut], w2[:, f, :], start=False, stop=f == NF - 1)
                last.then_inc(down_done, 1)

            def ffn2_up(n, par, f):
                if f == 0:
                    pe.wait_ge(ffn_lo, n + 1)
                pe.wait_ge(gelu_done, n * NF + (f - (NF - 1)))
                o = ps_up2[f][:]
                pe.matmul(o, w1[:, f * P:(f + 1) * P], xnT_hi[:, par, :], start=True, stop=False)
                pe.matmul(o, w1[:, f * P:(f + 1) * P], xnT_lo[:, par, :], start=False, stop=True)\
                    .then_inc(up_done, 1)

            def ffn2_down(n, i, par, half):
                if half == 0:
                    pe.wait_ge(hid_lo2, i * (NF - 1) + (NF - 1))
                    pe.wait_ge(gelu_done, n * NF + NF)
                    pe.wait_ge(resid_done, n)
                for t in (2 * half, 2 * half + 1):
                    o = ps_down[:, t * P:(t + 1) * P]
                    cut = slice(t * P, (t + 1) * P)
                    pe.matmul(o, ones_b[:], brow[:, MIX_C:MIX_C + D], start=True, stop=False)
                    for f in range(NF - 1):
                        pe.matmul(o, h_hi[:, par, f, cut], w2[:, f, :], start=False, stop=False)
                        pe.matmul(o, h_lo[:, par, f, cut], w2[:, f, :], start=False, stop=False)
                    last = pe.matmul(o, h_last[:, par, cut], w2_last[:], start=False, stop=True)
                if half == 1:
                    last.then_inc(down_done, 1)

            def mix_transpose(i, par):
                pe.wait_ge(mix_normed, i + 1)
                after(pe, mix_lo, i)
                for t in range(T4):
                    last = pe.transpose(ps_inT[:, t * P:(t + 1) * P], xin[:, par, t, :], ident[:])
                last.then_inc(mix_T, 1)

            def mix_project(j, par, pair):
                if pair == 0:
                    pe.wait_ge(mix_lo, j + 1)
                after(pe, xv_done, j * 2 + (pair - 1))
                for a in range(2):
                    o = ps_mix[pair][:, a * MIX_C:(a + 1) * MIX_C]
                    pe.matmul(o, ones_b[:], brow[:, 0:MIX_C], start=True, stop=False)
                    for k in range(K):
                        at = par * BT + (2 * pair + a) * P + k
                        hi, lo = xinT_hi[:, at:at + P], xinT_lo[:, at:at + P]
                        pe.matmul(o, hi, wk_hi[:, k, :], start=False, stop=False)
                        pe.matmul(o, hi, wk_lo[:, k, :], start=False, stop=False)
                        last = pe.matmul(o, lo, wk_hi[:, k, :], start=False, stop=k == K - 1)
                last.then_inc(mix_mm, 1)

            def mix_project_x2(j, par):
                after(pe, x2_stored, j)
                cut = slice(2 + par * BT, 2 + (par + 1) * BT)
                pe.matmul(ps_x2[:], wx2_hi[:], xinT_hi[:, cut], start=True, stop=False)
                pe.matmul(ps_x2[:], wx2_hi[:], xinT_lo[:, cut], start=False, stop=False)
                pe.matmul(ps_x2[:], wx2_lo[:], xinT_hi[:, cut], start=False, stop=True).then_inc(x2_mm, 1)

            ffn_transpose(0, 0)
            pe.wait_ge(w1_ready, 1)

            def step(i, par, known):
                if known == 2:
                    pe.wait_ge(weights_ready, 1)
                    pe.wait_ge(v_ready, 4)
                ffn_up(i, par, 0)
                ffn_up(i, par, 1)
                if known is None or known >= 2:
                    mix_project(i - 2, par, 0)
                if known != NB - 1:
                    ffn_transpose(i + 1, 1 - par)
                ffn_up(i, par, 2)
                ffn_up(i, par, 3)
                if known is None or known >= 2:
                    mix_project_x2(i - 2, par)
                    mix_project(i - 2, par, 1)
                if known == 0:
                    impulse_responses()
                    pe.wait_ge(w2_ready, 1)
                    pe.wait_ge(bias_ready, 1)
                if known == 1:
                    pe.wait_ge(v_ready, 1)
                if known != 0:
                    mix_transpose(i - 1, 1 - par)
                ffn_down(i, par)
                if known == 0:
                    transpose_powers()

            each_block(pe, step, 4)
            for j in (NB - 2, NB - 1):
                if j == NB - 1:
                    mix_transpose(j, 1)
                mix_project(j, j % 2, 0)
                mix_project_x2(j, j % 2)
                mix_project(j, j % 2, 1)

            pe.wait_ge(xv_done, 2 * NB)
            pe.wait_ge(resid_done, NB)

            def group_rhs(g):
                return xv[:, bass.ds(g * DG, DG), :].rearrange("p a b -> p (a b)")

            def conv_state(g, s):
                pe.wait_ge(tab_ready, g + 1)
                after(pe, masked_done, g - 1)
                pe.matmul(ps_state[s % 2][:], vs[:, s, :], group_rhs(g), start=True, stop=True)\
                    .then_inc(state_mm, 1)

            def conv_from_states(g, s):
                pe.wait_ge(carry_ready, g + 1)
                after(pe, y_stored, g - 1)
                pe.matmul(ps_conv[s % 2][:], qs[:, s, :], gm[:, s % 2, :, :].rearrange("p d t -> p (d t)"),
                          start=True, stop=True, skip_group_check=True)

            def conv_in_chunk(g, s, turn):
                pe.wait_ge(toeplitz_loaded[s], turn * 16 + 16)
                for c in range(DG):
                    last = pe.matmul(ps_conv[s % 2][:, c * TILES:(c + 1) * TILES], ring[:, s, c, :],
                                     xv[:, bass.ds(g * DG + c, 1), :].rearrange("p a b -> p (a b)"),
                                     start=False, stop=True, skip_group_check=True)
                last.then_inc(conv_mm, 1)

            def conv_turn(turn, last_turn=False):
                for s in range(4):
                    conv_from_states(turn * 4 + s, s)
                    if not (last_turn and s >= 2):
                        conv_state(turn * 4 + (s + 2), (s + 2) % 4)
                    conv_in_chunk(turn * 4 + s, s, turn)

            conv_state(0, 0)
            conv_state(1, 1)
            conv_turn(0)
            with pe.Fori(1, NGR // 4 - 1) as turn:
                conv_turn(turn)
            conv_turn(NGR // 4 - 1, True)

            def y_transpose(i, par):
                pe.wait_ge(y_staged, i + 1)
                after(pe, gated, i)
                for t in range(T4):
                    last = pe.transpose(ps_yT[:, t * P:(t + 1) * P], yst[:, par, t, :], flip[:])
                last.then_inc(y_T, 1)

            def project_out(i, par):
                pe.wait_ge(gated, i + 1)
                after(pe, y_sum, i)
                for t in range(T4):
                    last = pe.matmul(ps_proj[:, t * P:(t + 1) * P], yxT[:, par, t * P:(t + 1) * P], wo[:],
                                     start=True, stop=True)
                last.then_inc(proj_mm, 1)

            def z_transpose(i, par):
                pe.wait_ge(z_ready, i + 1)
                after(pe, z_lo, i)
                for t in range(T4):
                    last = pe.transpose(ps_zT[:, t * P:(t + 1) * P], zm[:, par, t, :], ident[:])
                last.then_inc(z_T, 1)

            def gate_up(i, par, f):
                if f == 0:
                    pe.wait_ge(z_lo, i + 1)
                b = (NG * par + f) % 2
                after(pe, glu_done, i * NG + (f - 1))
                for m, ps in ((f, ps_l1[b]), (NG + f, ps_l2[b])):
                    o = ps[0:GP, :]
                    pe.matmul(o, l12_hi[:, m, :], zT_hi[:, par, :], start=True, stop=False)
                    pe.matmul(o, l12_hi[:, m, :], zT_lo[:, par, :], start=False, stop=False)
                    last = pe.matmul(o, l12_lo[:, m, :], zT_hi[:, par, :], start=False, stop=True)
                last.then_inc(l12_mm, 1)

            def gate_down(i, par):
                pe.wait_ge(glu_done, i * NG + NG)
                after(pe, mixed, i)
                for t in range(T4):
                    for f in range(NG):
                        last = pe.matmul(ps_l3[:, t * P:(t + 1) * P], gg[:, par, f, t * P:(t + 1) * P],
                                         l3[:, f, :], start=f == 0, stop=f == NG - 1)
                last.then_inc(l3_mm, 1)

            pe.wait_ge(masked_done, NGR)
            pe.wait_ge(y_stored, NGR)
            for i in range(2):
                y_transpose(i, i)
                project_out(i, i)
            z_transpose(0, 0)

            def step(i, par, known):
                gate_up(i, par, 0)
                if known is None or known < NB - 2:
                    y_transpose(i + 2, par)
                gate_up(i, par, 1)
                if known is None or known < NB - 2:
                    project_out(i + 2, par)
                if known != NB - 1:
                    z_transpose(i + 1, 1 - par)
                else:
                    ffn_transpose(NB, 0)
                if known != 0:
                    gate_down(i - 1, 1 - par)
                gate_up(i, par, 2)

            each_block(pe, step, 2)

            pe.wait_ge(w2_last_ready, 1)
            pe.wait_ge(y_sum, NB)

            def step(i, par, known):
                ffn2_up(i + NB, par, 0)
                if known == 0:
                    gate_down(NB - 1, 1)
                ffn2_up(i + NB, par, 1)
                if known != NB - 1:
                    ffn_transpose(i + (NB + 1), 1 - par)
                if known != 0:
                    ffn2_down(i + (NB - 1), i - 1, 1 - par, 0)
                ffn2_up(i + NB, par, 2)
                if known != 0:
                    ffn2_down(i + (NB - 1), i - 1, 1 - par, 1)
                ffn2_up(i + NB, par, 3)

            each_block(pe, step, 2)
            for half in range(2):
                ffn2_down(2 * NB - 1, NB - 1, 1, half)

        @block.scalar
        def _(act):
            act.wait_ge(ffn_w_loaded, 48)
            act.activation(tmp_a[:, 0:FF], w1s, ACT.Abs, accum_out=small[:, 0:1])
            act.activation(tmp_a[:, FF:2 * FF], w2s, ACT.Abs, accum_out=small[:, 1:2]).then_inc(abs_summed, 1)
            act.wait_ge(small_w_loaded, 64)
            act.wait_ge(sel_ready, 2)
            for g in range(NGR):
                act.activation(pow_t[:, g * P:(g + 1) * P], iota_t, ACT.Exp, scale=lp[:, g:g + 1])
            act.activation(decay[:], lp[:], ACT.Exp, scale=float(P)).then_inc(powers, 1)

            def copy_impulse():
                for q in range(4):
                    act.wait_ge(impulse_mm, q + 1)
                    act.activation(hp[:, q * BT:(q + 1) * BT], bank[4 + q][0:DG, :], ACT.Copy)\
                        .then_inc(impulse_copied, 1)

            def copy_powers():
                for q in range(4):
                    act.wait_ge(pow_T, q + 1)
                    act.activation(v_all[:, q * BT:(q + 1) * BT], bank[4 + q][:], ACT.Copy).then_inc(v_ready, 1)

            def ffn_split_hi(n, par):
                act.wait_ge(ffn_T, n + 1)
                act.activation(xnT_hi[:, par, :], ps_xnT[:], ACT.Copy).then_inc(ffn_hi, 1)

            def ffn_gelu(n, par, f):
                act.wait_ge(up_done, n * NF + f + 1)
                if f == 0:
                    after(act, hid0_lo, n)
                else:
                    after(act, hid_lo, n * (NF - 1) + (f - (NF - 1)))
                act.activation(h32[:, f, :], ps_up[f % 2][:], ACT.Gelu, bias=b1[:, f:f + 1])
                act.activation(h_hi[:, par, f, :], ps_up[f % 2][:], ACT.Gelu, bias=b1[:, f:f + 1])\
                    .then_inc(gelu_done, 1)

            def mix_split_hi(i, par):
                act.wait_ge(mix_T, i + 1)
                act.activation(xinT_hi[:, 2 + par * BT:2 + (par + 1) * BT], ps_inT[:], ACT.Copy)\
                    .then_inc(mix_hi, 1)

            def copy_v(j, pair):
                act.wait_ge(mix_mm, j * 2 + (pair + 1))
                after(act, xv_done, j * 2 + (pair - 1))
                act.activation(vt[:, pair, :, :], ps_mix[pair][:].rearrange("p (a c) -> p a c", a=2)[:, :, D:2 * D],
                               ACT.Copy).then_inc(v_copied, 1)

            def store_x2(j, par):
                act.wait_ge(x2_mm, j + 1)
                after(act, x2_done, j - par)
                act.activation(x2_raw[:, 2 + par * BT:2 + (par + 1) * BT], ps_x2[:], ACT.Copy)
                act.activation(x2T[:, bass.ds(j * BT, BT)], ps_x2[:], ACT.Identity, bias=sbx2[:, 0:1],
                               scale=tap_x2[:, K - 1:K]).then_inc(x2_stored, 1)

            ffn_split_hi(0, 0)

            def step(i, par, known):
                ffn_gelu(i, par, 0)
                ffn_gelu(i, par, 1)
                if known is None or known >= 2:
                    copy_v(i - 2, 0)
                if known != NB - 1:
                    ffn_split_hi(i + 1, 1 - par)
                ffn_gelu(i, par, 2)
                ffn_gelu(i, par, 3)
                if known is None or known >= 2:
                    store_x2(i - 2, par)
                    copy_v(i - 2, 1)
                if known == 0:
                    copy_impulse()
                    copy_powers()
                if known != 0:
                    mix_split_hi(i - 1, 1 - par)

            each_block(act, step, 4)
            for j in (NB - 2, NB - 1):
                if j == NB - 1:
                    mix_split_hi(j, 1)
                copy_v(j, 0)
                store_x2(j, j % 2)
                copy_v(j, 1)

            def store_y(g, s):
                act.wait_ge(conv_mm, g + 1)
                act.activation(xv[:, bass.ds(g * DG, DG), :],
                               ps_conv[s % 2][:].rearrange("p (c t) -> p c t", c=DG), ACT.Copy).then_inc(y_stored, 1)

            with act.Fori(0, NGR // 2) as turn:
                for s in range(2):
                    store_y(turn * 2 + s, s)

            def square(i, par):
                act.wait_ge(y_sum, i + 1)
                after(act, z_T, i - 1)
                for t in range(T4):
                    last = act.activation(zm[:, par, t, :], y_sb[:, par, t, :], ACT.Square,
                                          accum_out=ss[:, par, t:t + 1])
                last.then_inc(squared, 1)

            def z_split_hi(i, par):
                act.wait_ge(z_T, i + 1)
                act.activation(zT_hi[:, par, :], ps_zT[:], ACT.Copy).then_inc(z_hi, 1)

            def gate_gelu(i, par, f):
                b = (NG * par + f) % 2
                act.wait_ge(l12_mm, i * NG + (f + 1))
                after(act, glu_done, i * NG + (f - 1))
                act.activation(g1[:, b, :], ps_l1[b][0:GP, :], ACT.Gelu_apprx_tanh).then_inc(g1_done, 1)

            square(0, 0)
            square(1, 1)
            z_split_hi(0, 0)

            def step(i, par, known):
                gate_gelu(i, par, 0)
                gate_gelu(i, par, 1)
                if known != NB - 1:
                    z_split_hi(i + 1, 1 - par)
                else:
                    ffn_split_hi(NB, 0)
                if known is None or known < NB - 2:
                    square(i + 2, par)
                gate_gelu(i, par, 2)

            each_block(act, step, 2)

            act.wait_ge(gated, NB)

            def ffn2_gelu(n, i, par, f, known):
                act.wait_ge(up_done, n * NF + f + 1)
                if f == NF - 1:
                    act.activation(h_last[:, par, :], ps_up2[f][:], ACT.Gelu, bias=b1[:, f:f + 1])\
                        .then_inc(gelu_done, 1)
                    return
                if known != 0:
                    act.wait_ge(hid_lo2, i * (NF - 1) + (f - 2))
                act.activation(h32[:, f, :], ps_up2[f][:], ACT.Gelu, bias=b1[:, f:f + 1])
                act.activation(h_hi[:, par, f, :], ps_up2[f][:], ACT.Gelu, bias=b1[:, f:f + 1])\
                    .then_inc(gelu_done, 1)

            def step(i, par, known):
                ffn2_gelu(i + NB, i, par, 0, known)
                ffn2_gelu(i + NB, i, par, 1, known)
                if known != NB - 1:
                    ffn_split_hi(i + (NB + 1), 1 - par)
                ffn2_gelu(i + NB, i, par, 2, known)
                ffn2_gelu(i + NB, i, par, 3, known)

            each_block(act, step, 2)

        @block.vector
        def _(dve):
            chain = [0]

            def link(ins):
                chain[0] += 1
                ins.then_inc(dve_step, 1)
                dve.wait_ge(dve_step, chain[0])

            dve.memset(ones_b[:], 1.0)
            dve.memset(ones_f[:], 1.0).then_inc(consts, 1)
            dve.memset(carry[:], 1.0)
            dve.memset(xinT_hi[:, 0:2], 0.0)
            dve.memset(xinT_lo[:, 0:2], 0.0)
            dve.memset(x2_raw[:, 0:2], 0.0)
            link(dve.memset(zeros, 0.0))
            dve.memset(carry[:].rearrange("p (b c) -> p b c", b=B)[:, :, 0:1], 0.0).then_inc(zeros_ready, 1)

            def ternary_weights():
                below = tmp_a[:, 2 * FF:4 * FF]
                dve.wait_ge(abs_total, 1)
                link(dve.tensor_scalar(small[:, 2:4], ps_x2[:, 0:2], 1.0 / (D * FF), 1e-8, ALU.mult, ALU.max))
                dve.tensor_scalar(small[:, 4:6], small[:, 2:4], 0.5, None, ALU.mult)
                link(dve.tensor_scalar(small[:, 6:8], small[:, 2:4], -0.5, None, ALU.mult))
                link(dve.tensor_scalar(below[:, 0:FF], w1s, small[:, 6:7], None, ALU.is_lt))
                dve.scalar_tensor_tensor(w1[:], w1s, small[:, 4:5], below[:, 0:FF], ALU.is_gt, ALU.subtract)\
                    .then_inc(w1_ready, 1)
                link(dve.tensor_scalar(below[:, FF:2 * FF], w2s, small[:, 7:8], None, ALU.is_lt))
                dve.scalar_tensor_tensor(w2[:].rearrange("p f d -> p (f d)"), w2s, small[:, 5:6],
                                         below[:, FF:2 * FF], ALU.is_gt, ALU.subtract).then_inc(w2_ready, 1)

            def bias_parts():
                nbr = MIX_C + D
                cols = iter(setup_a[:, 4608 + n * nbr:4608 + (n + 1) * nbr] for n in range(4))
                rest, acc, acc2 = next(cols), next(cols), next(cols)
                part = next(cols).bitcast(BF16)[:, 0:nbr]
                dve.wait_ge(small_w_loaded, 64)
                dve.wait_ge(sel_ready, 2)
                link(dve.tensor_copy(part, brs))
                dve.tensor_tensor(rest, brs, part, ALU.subtract)
                link(dve.tensor_scalar(acc, part, ident[:, 0:1], None, ALU.mult))
                link(dve.tensor_copy(part, rest))
                link(dve.tensor_tensor(rest, rest, part, ALU.subtract))
                link(dve.scalar_tensor_tensor(acc2, part, ident[:, 1:2], acc, ALU.mult, ALU.add))
                dve.scalar_tensor_tensor(brow[:], rest, ident[:, 2:3], acc2, ALU.mult, ALU.add)\
                    .then_inc(bias_ready, 1)

            def pole_weights():
                sel_rows = sel[:].unsqueeze(1).to_broadcast([P, NGR, DG])
                dve.tensor_tensor(sel_res[:], sel_rows, res[:].unsqueeze(2).to_broadcast([P, NGR, DG]), ALU.mult)\
                    .then_inc(sel_res_ready, 1)
                dve.wait_ge(powers, 1)
                pow3 = pow_t.rearrange("p (g t) -> p g t", g=NGR)
                link(dve.tensor_tensor(rp[:].unsqueeze(2), res[:].unsqueeze(2), pow3[:, :, P - 2:P - 1], ALU.mult))
                dve.tensor_tensor(sel_rp[:], sel_rows, rp[:].unsqueeze(2).to_broadcast([P, NGR, DG]), ALU.mult)

            def mixer_weights():
                wprime, wk = tmp_a[:, 0:3 * D], tmp_a[:, 512:512 + K * MIX_C]
                dve.wait_ge(mix_w_loaded, 9 * 16)
                link(dve.tensor_scalar(wprime, wins, prew[:, 0:1], None, ALU.mult))
                dve.tensor_copy(wx2_hi[:], wprime[:, 0:D])
                wk3 = wk.rearrange("p (k c) -> p k c", k=K)
                link(dve.tensor_tensor(wk3, wprime[:, D:3 * D].unsqueeze(1).to_broadcast([P, K, MIX_C]),
                                       srows.rearrange("p (k c) -> p k c", k=K), ALU.mult))
                dve.tensor_tensor(wx2_lo[:], wprime[:, 0:D], wx2_hi[:], ALU.subtract)
                link(dve.tensor_copy(wk_hi[:], wk3))
                dve.tensor_tensor(wk_lo[:], wk3, wk_hi[:], ALU.subtract)
                link(dve.tensor_scalar(l12s, l12s, postw[:, 0:1], None, ALU.mult))
                l12v = l12s.rearrange("p (m c) -> p m c", m=2 * NG)
                link(dve.tensor_copy(l12_hi[:], l12v))
                dve.tensor_tensor(l12_lo[:], l12v, l12_hi[:], ALU.subtract).then_inc(weights_ready, 1)
                newest = hp.rearrange("p (g w) -> p g w", g=NGR)[:, :, P - 1:P]
                dve.wait_ge(impulse_copied, 4)
                dve.tensor_tensor(newest, newest, dsk[:].unsqueeze(2), ALU.add).then_inc(impulse_ready, 1)

            def stats(n, par, buf, agg, sems, tile_block, rms):
                half, square, out_sem = sems
                for t in range(T4):
                    last = dve.bn_stats(buf[:, par, t, 0:6], xres[:, bass.ds(tile_block * T4 + t, 1), :]
                                        .rearrange("p a d -> p (a d)"))
                last.then_inc(half, 1)
                b, m = buf[:, par], agg[:, par]
                dve.wait_ge(half, n + 1)
                dve.tensor_tensor(m[:, 2, :], b[:, :, 1], b[:, :, 4], ALU.add)
                dve.tensor_tensor(m[:, 3, :], b[:, :, 1], b[:, :, 4], ALU.subtract)
                if rms:
                    dve.tensor_tensor(m[:, 4, :], b[:, :, 2], b[:, :, 5], ALU.add).then_inc(square, 1)
                else:
                    dve.scalar_tensor_tensor(m[:, 4, :], b[:, :, 2], D * LN_EPS, b[:, :, 5], ALU.add, ALU.add)\
                        .then_inc(square, 1)
                steps = 3 if rms else 2
                dve.wait_ge(square, n * steps + 1)
                dve.tensor_scalar(m[:, 0, :], m[:, 2, :], -0.5, None, ALU.mult)
                dve.scalar_tensor_tensor(m[:, 5, :], m[:, 3, :], 0.25, m[:, 3, :], ALU.mult, ALU.mult)\
                    .then_inc(square, 1)
                dve.wait_ge(square, n * steps + 2)
                last = dve.scalar_tensor_tensor(m[:, 1, :], m[:, 4, :], 1.0 / D, m[:, 5, :], ALU.mult, ALU.add)
                if rms:
                    last.then_inc(square, 1)
                    dve.wait_ge(square, n * steps + 3)
                    dve.tensor_scalar(m[:, 6, :], m[:, 1, :], LN_EPS, None, ALU.add)
                    last = dve.tensor_scalar(m[:, 7, :], m[:, 1, :], 1.0 + RMS_EPS, RMS_EPS * LN_EPS, ALU.mult,
                                             ALU.add)
                last.then_inc(out_sem, 1)

            def ffn_stat(n, i, par):
                after(dve, ffn_normed, n - 1)
                stats(n, par, bnst, mv, (ffn_bn, ffn_square, ffn_stats), i, rms=False)

            def ffn_split_lo(n, par):
                dve.wait_ge(ffn_hi, n + 1)
                dve.tensor_tensor(xnT_lo[:, par, :], ps_xnT[:], xnT_hi[:, par, :], ALU.subtract).then_inc(ffn_lo, 1)

            def hidden_lo(n, par, f):
                dve.wait_ge(gelu_done, n * NF + f + 1)
                dve.tensor_tensor(h_lo[:, par, f, :], h32[:, f, :], h_hi[:, par, f, :], ALU.subtract)\
                    .then_inc(hid_lo, 1)

            def ffn_residual(n, i):
                dve.wait_ge(down_done, n + 1)
                xb = tiles_of(xres, i).rearrange("p t d -> p (t d)")
                dve.scalar_tensor_tensor(xb, ps_down[:], 0.5, xb, ALU.mult, ALU.add).then_inc(resid_done, 1)

            def mix_stat(i, par):
                stats(i, par, bnst2, mv2, (mix_bn, mix_square, mix_stats), i, rms=True)

            def mix_split_lo(i, par):
                dve.wait_ge(mix_hi, i + 1)
                cut = slice(2 + par * BT, 2 + (par + 1) * BT)
                dve.tensor_tensor(xinT_lo[:, cut], ps_inT[:], xinT_hi[:, cut], ALU.subtract).then_inc(mix_lo, 1)

            def gate_x1_v(j, pair):
                dve.wait_ge(v_copied, j * 2 + (pair + 1))
                dve.tensor_tensor(xv[:, :, bass.ds(j * T4 + 2 * pair, 2)],
                                  ps_mix[pair][:].rearrange("p (a c) -> p c a", a=2)[:, 0:D, :],
                                  vt[:, pair, :, :].rearrange("p a c -> p c a"), ALU.mult).then_inc(xv_done, 1)

            def filter_x2(j, par):
                now = x2T[:, bass.ds(j * BT, BT)]
                dve.wait_ge(x2_stored, j + 1)
                for k, done in ((1, x2_tap), (0, x2_done)):
                    at = par * BT + k
                    dve.scalar_tensor_tensor(now, x2_raw[:, at:at + BT], tap_x2[:, k:k + 1], now, ALU.mult, ALU.add)\
                        .then_inc(done, 1)
                    if k == 1:
                        dve.wait_ge(x2_tap, j + 1)

            dve.wait_ge(x_loaded, 16)
            ffn_stat(0, 0, 0)
            ternary_weights()
            ffn_split_lo(0, 0)
            dve.wait_ge(x_loaded, 32)
            ffn_stat(1, 1, 1)
            bias_parts()
            pole_weights()

            def step(i, par, known):
                hidden_lo(i, par, 1)
                if known is None or known >= 2:
                    gate_x1_v(i - 2, 0)
                if known != NB - 1:
                    ffn_split_lo(i + 1, 1 - par)
                if known is None or known < NB - 2:
                    dve.wait_ge(x_loaded, i * 16 + 48)
                    ffn_stat(i + 2, i + 2, par)
                hidden_lo(i, par, 2)
                hidden_lo(i, par, 3)
                if known is None or known >= 2:
                    filter_x2(i - 2, par)
                    gate_x1_v(i - 2, 1)
                if known != 0:
                    mix_split_lo(i - 1, 1 - par)
                if known == 1:
                    mixer_weights()
                ffn_residual(i, i)
                after(dve, mix_normed, i - 1)
                dve.wait_ge(resid_done, i + 1)
                dve.tensor_copy(mv2[:, par, 2, :], ones_f[:, 0:T4])
                mix_stat(i, par)

            each_block(dve, step, 4)
            for j in (NB - 2, NB - 1):
                if j == NB - 1:
                    mix_split_lo(j, 1)
                gate_x1_v(j, 0)
                filter_x2(j, j % 2)
                gate_x1_v(j, 1)

            mask_cols = sel[:].unsqueeze(2).to_broadcast([P, DG, TILES])
            dve.wait_ge(hid_lo, (NF - 1) * NB)
            dve.wait_ge(hid0_lo, NB)
            dve.wait_ge(down_done, NB)
            dve.memset(gm, 0.0).then_inc(dve_step, 1)
            chain[0] += 1
            dve.wait_ge(dve_step, chain[0])

            def carry_states(g, s):
                par = s % 2
                dve.tensor_scalar(dk[:, par, :], carry[:], decay[:, bass.ds(g, 1)], None, ALU.mult)\
                    .then_inc(decay_ready, 1)
                dve.wait_ge(state_mm, g + 1)
                dve.tensor_tensor(masked, ps_state[par][:].rearrange("p (c t) -> p c t", c=DG), mask_cols, ALU.mult)\
                    .then_inc(masked_done, 1)
                dve.wait_ge(masked_done, g + 1)
                dve.tensor_reduce(ssum[:, par, :], masked.rearrange("p c t -> p t c"), AX_X, ALU.add)\
                    .then_inc(summed, 1)
                dve.wait_ge(summed, g + 1)
                dve.wait_ge(decay_ready, g + 1)
                dve.tensor_tensor_scan(state[:, par, :], dk[:, par, :], ssum[:, par, :], 0.0, ALU.mult, ALU.add)\
                    .then_inc(scanned, 1)
                dve.wait_ge(scanned, g + 1)
                after(dve, conv_mm, g - 1)
                before = state[:, par, :].rearrange("p (b c) -> p b c", b=B)[:, :, 0:CH - 1]
                rp_cols = sel_rp[:, bass.ds(g, 1), :].rearrange("p a c -> p (a c)")
                into = gm[:, par, :, :].rearrange("p d (b c) -> p d b c", b=B)[:, :, :, 1:CH]
                dve.tensor_tensor(into, before.unsqueeze(1).to_broadcast([P, DG, B, CH - 1]),
                                  rp_cols.unsqueeze(2).unsqueeze(3).to_broadcast([P, DG, B, CH - 1]), ALU.mult)\
                    .then_inc(carry_ready, 1)

            for g in range(2):
                carry_states(g, g)
            with dve.Fori(1, NGR // 2) as turn:
                for s in range(2):
                    carry_states(turn * 2 + s, s)

            def stage_y(i, par):
                after(dve, y_T, i - 1)
                dve.tensor_copy(yst[:, par, :, :], xv[:, :, bass.ds(i * T4, T4)].rearrange("p d t -> p t d"))\
                    .then_inc(y_staged, 1)

            def gate_y(i, par):
                dve.wait_ge(y_T, i + 1)
                after(dve, proj_mm, i - 1)
                dve.tensor_tensor(yxT[:, par, :], ps_yT[:], x2T[:, bass.ds(i * BT, BT)], ALU.mult)\
                    .then_inc(gated, 1)

            def sum_y(i, par):
                dve.wait_ge(proj_mm, i + 1)
                dve.wait_ge(u_ready, i + 1)
                after(dve, xy_done, i - 1)
                dve.tensor_tensor(y_sb[:, par, :, :], ps_proj[:].rearrange("p (t d) -> p t d", t=T4),
                                  u_sb[:, par, :, :], ALU.add).then_inc(y_sum, 1)

            def z_split_lo(i, par):
                dve.wait_ge(z_hi, i + 1)
                dve.tensor_tensor(zT_lo[:, par, :], ps_zT[:], zT_hi[:, par, :], ALU.subtract).then_inc(z_lo, 1)

            def glu(i, par, f):
                b = (NG * par + f) % 2
                dve.wait_ge(g1_done, i * NG + (f + 1))
                if f == 0:
                    after(dve, l3_mm, i - 1)
                dve.tensor_tensor(gg[:, par, f, :], ps_l2[b][0:GP, :], g1[:, b, :], ALU.mult).then_inc(glu_done, 1)

            def mixer_residual(i):
                dve.wait_ge(l3_mm, i + 1)
                dve.wait_ge(xy_done, i + 1)
                xb = tiles_of(xres, i).rearrange("p t d -> p (t d)")
                dve.tensor_tensor(xb, ps_l3[:], xb, ALU.add).then_inc(mixed, 1)

            dve.wait_ge(y_stored, NGR)
            stage_y(0, 0)
            stage_y(1, 1)
            for i in range(2):
                gate_y(i, i)
                sum_y(i, i)
            stage_y(2, 0)
            z_split_lo(0, 0)

            def step(i, par, known):
                if known in (NB - 2, NB - 1):
                    dve.wait_ge(mixed, 2)
                    ffn_stat(i + 2, i - (NB - 2), par)
                if known is None or known < NB - 3:
                    stage_y(i + 3, 1 - par)
                if known is None or known < NB - 2:
                    gate_y(i + 2, par)
                glu(i, par, 0)
                glu(i, par, 1)
                if known is None or known < NB - 2:
                    sum_y(i + 2, par)
                if known != NB - 1:
                    z_split_lo(i + 1, 1 - par)
                else:
                    ffn_split_lo(NB, 0)
                if known != 0:
                    mixer_residual(i - 1)
                glu(i, par, 2)

            each_block(dve, step, 2, 4)
            mixer_residual(NB - 1)

            def hidden_lo2(n, par, f):
                dve.wait_ge(gelu_done, n * NF + f + 1)
                dve.tensor_tensor(h_lo[:, par, f, :], h32[:, f, :], h_hi[:, par, f, :], ALU.subtract)\
                    .then_inc(hid_lo2, 1)

            def step(i, par, known):
                if known is None or known < NB - 2:
                    dve.wait_ge(mixed, i + 3)
                    ffn_stat(i + (NB + 2), i + 2, par)
                hidden_lo2(i + NB, par, 0)
                if known != NB - 1:
                    ffn_split_lo(i + (NB + 1), 1 - par)
                hidden_lo2(i + NB, par, 1)
                if known != 0:
                    ffn_residual(i + (NB - 1), i - 1)
                hidden_lo2(i + NB, par, 2)

            each_block(dve, step, 2)
            ffn_residual(2 * NB - 1, NB - 1)

        @block.gpsimd
        def _(pool):
            pool.memset(mhalf[:], -0.5)
            pool.memset(rms_eps[:], RMS_EPS)
            pool.memset(inv_d[:], 1.0 / D)
            pool.memset(sel[:], 1.0)
            pool.memset(flip[:], 0.0)
            pool.memset(ident[:], 0.0).then_inc(cleared, 1)
            pool.wait_ge(cleared, 1)
            pool.affine_select(ident[:], ident[:], pattern=[[-1, P]], compare_op=ALU.not_equal, fill=1.0,
                               base=0, channel_multiplier=1)
            pool.affine_select(flip[:], flip[:], pattern=[[1, P]], compare_op=ALU.not_equal, fill=1.0,
                               base=1 - P, channel_multiplier=1)
            pool.iota(iota_t, pattern=[[-1, P]], base=P - 1, channel_multiplier=0, allow_small_or_imprecise_dtypes=True)
            pool.affine_select(sel[:], sel[:], pattern=[[-S, DG]], compare_op=ALU.is_ge, fill=0.0,
                               base=0, channel_multiplier=1).then_inc(sel_ready, 1)
            pool.wait_ge(sel_ready, 1)
            pool.affine_select(sel[:], sel[:], pattern=[[S, DG]], compare_op=ALU.is_ge, fill=0.0,
                               base=S - 1, channel_multiplier=-1).then_inc(sel_ready, 1)

            def ffn_norm(n, i, par):
                pool.wait_ge(ffn_stats, n + 1)
                after(pool, ffn_T, n - 1)
                pool.tensor_tensor(fs[:, par, :], mv[:, par, 1, :], mhalf[:, 0, :], ALU.pow)
                pool.tensor_tensor(xn[:, par, :, :], tiles_of(xres, i), per_tile(mv[:, par, 0, :]), ALU.add)\
                    .then_inc(ffn_centred, 1)
                pool.wait_ge(ffn_centred, n + 1)
                pool.tensor_tensor(xn[:, par, :, :], xn[:, par, :, :], per_tile(fs[:, par, :]), ALU.mult)\
                    .then_inc(ffn_normed, 1)

            def mix_norm(i, par):
                cols = bass.ds(i * T4, T4)
                negm = mv2[:, par, 0, :]
                pool.wait_ge(mix_stats, i + 1)
                after(pool, mix_T, i - 1)
                pool.tensor_tensor(ms[:, par, :, :], mv2[:, par, 6:8, :], mhalf[:], ALU.pow)
                pool.tensor_tensor(xin[:, par, :, :], tiles_of(xres, i), per_tile(negm), ALU.add)
                pool.tensor_copy(negm1[:, cols], negm).then_inc(mix_step, 1)
                pool.wait_ge(mix_step, i + 1)
                pool.tensor_copy(rstd1[:, cols], ms[:, par, 0, :])
                pool.tensor_tensor(xin[:, par, :, :], xin[:, par, :, :], per_tile(ms[:, par, 1, :]), ALU.mult)\
                    .then_inc(mix_normed, 1)

            def hidden0_lo(n, par):
                pool.wait_ge(gelu_done, n * NF + 1)
                pool.tensor_tensor(h_lo[:, par, 0, :], h32[:, 0, :], h_hi[:, par, 0, :], ALU.subtract)\
                    .then_inc(hid0_lo, 1)

            ffn_norm(0, 0, 0)
            ffn_norm(1, 1, 1)
            pool.wait_ge(w2_ready, 1)
            pool.tensor_copy(w2_last[:], w2[:, NF - 1, :]).then_inc(w2_last_ready, 1)

            def step(i, par, known):
                hidden0_lo(i, par)
                if known != 0:
                    mix_norm(i - 1, 1 - par)
                if known is None or known < NB - 2:
                    ffn_norm(i + 2, i + 2, par)

            each_block(pool, step, 4)
            mix_norm(NB - 1, 1)

            def stage_tables(g, s):
                after(pool, conv_mm, g - 3)
                pool.tensor_copy(vs[:, s, :], v_all[:, bass.ds(g * P, P)])
                pool.tensor_copy(qs[:, s, :], pow_t[:, bass.ds(g * P, P)]).then_inc(tab_ready, 1)

            pool.wait_ge(powers, 1)
            pool.wait_ge(v_ready, 4)
            for g in range(4):
                stage_tables(g, g)
            with pool.Fori(1, NGR // 4) as turn:
                for s in range(4):
                    stage_tables(turn * 4 + s, s)

            def make_u(i, par):
                cols = bass.ds(i * T4, T4)
                after(pool, y_sum, i - 1)
                pool.tensor_tensor(u_sb[:, par, :, :], tiles_of(xres, i), per_tile(negm1[:, cols]), ALU.add)\
                    .then_inc(u_centred, 1)
                pool.wait_ge(u_centred, i + 1)
                pool.tensor_tensor(u_sb[:, par, :, :], u_sb[:, par, :, :], per_tile(rstd1[:, cols]), ALU.mult)\
                    .then_inc(u_ready, 1)

            def z_norm(i, par):
                pool.wait_ge(squared, i + 1)
                pool.tensor_tensor(rr[:, par, 0, :], ss[:, par, :], inv_d[:], ALU.mult).then_inc(z_var, 1)
                pool.wait_ge(z_var, i * 2 + 1)
                pool.tensor_tensor(rr[:, par, 1, :], rr[:, par, 0, :], rms_eps[:], ALU.add).then_inc(z_var, 1)
                pool.wait_ge(z_var, i * 2 + 2)
                pool.tensor_tensor(rr[:, par, 2, :], rr[:, par, 1, :], mhalf[:, 0, :], ALU.pow).then_inc(z_rstd, 1)
                pool.wait_ge(z_rstd, i + 1)
                pool.tensor_tensor(zm[:, par, :, :], y_sb[:, par, :, :], per_tile(rr[:, par, 2, :]), ALU.mult)\
                    .then_inc(z_ready, 1)
                pool.tensor_tensor(tiles_of(xres, i), tiles_of(xres, i), y_sb[:, par, :, :], ALU.add)\
                    .then_inc(xy_done, 1)

            pool.wait_ge(tab_ready, NGR)
            make_u(0, 0)
            make_u(1, 1)
            z_norm(0, 0)
            z_norm(1, 1)
            make_u(2, 0)

            def step(i, par, known):
                if known is None or known < NB - 2:
                    z_norm(i + 2, par)
                if known is None or known < NB - 3:
                    make_u(i + 3, 1 - par)

            each_block(pool, step, 2, 4)

            pool.wait_ge(z_T, NB - 1)
            ffn_norm(NB, 0, 0)
            pool.wait_ge(z_T, NB)
            ffn_norm(NB + 1, 1, 1)

            def step(i, par, known):
                if known is None or known < NB - 2:
                    ffn_norm(i + (NB + 2), i + 2, par)

            each_block(pool, step, 2)


def kernel(**inputs):
    import numpy as np
    import concourse.bacc as _bacc
    from concourse.bass_utils import run_bass_kernel_spmd as _run

    def arr(name):
        return np.asarray(inputs["L0_" + name])

    def rows(a):
        return np.broadcast_to(a.reshape(1, -1), (P, a.size))

    short = arr("attn_short_w").reshape(3 * D, K)
    short_b, b2 = arr("attn_short_b"), arr("ffn_b2")
    l12 = np.concatenate([arr("attn_l1_w"), arr("attn_l2_w")], axis=0)
    data = {
        "x": arr("attn_u").reshape(TILES, P, D).transpose(1, 0, 2),
        "w1t": arr("ffn_W1").T,
        "b1c": arr("ffn_b1").reshape(NF, P).T,
        "w2t": arr("ffn_W2").T.reshape(NF, P, D).transpose(1, 0, 2).reshape(P, NF * D),
        "bias_rows": rows(np.concatenate([short_b[D:], b2])),
        "pre_w": arr("attn_pre_norm_w").reshape(P, 1),
        "wint": arr("attn_in_proj_w").T,
        "short_rows": rows(short[D:].T),
        "short_x2": short[:D],
        "short_bc": short_b[:D].reshape(P, 1),
        "poles": arr("attn_log_poles").reshape(NGR, P).T,
        "residues": arr("attn_residues").reshape(NGR, P).T,
        "dskip": arr("attn_D_skip").reshape(NGR, DG).T,
        "wot": arr("attn_out_proj_w").T,
        "post_w": arr("attn_post_norm_w").reshape(P, 1),
        "l12t": l12.T,
        "l3t": arr("attn_l3_w").T.reshape(NG, GP, D).transpose(1, 0, 2),
    }
    nc = _bacc.Bacc("TRN2", target_bir_lowering=False, num_devices=1)
    arrays, args = {}, []
    for name, a in data.items():
        arrays[name] = np.ascontiguousarray(a)
        args.append(nc.dram_tensor(name, a.shape, F32, kind="ExternalInput").ap())
    args.append(nc.dram_tensor("out", (P, TILES, D), F32, kind="ExternalOutput").ap())
    macaron_kernel(nc, *args)
    r = _run(nc, [arrays], core_ids=[0])
    got = np.asarray(r.results[0]["out"])
    return np.ascontiguousarray(got.transpose(1, 0, 2)).reshape(B, L, D)
```

```python
from contextlib import ExitStack

import concourse.bass as bass
from concourse import mybir

F32 = mybir.dt.float32
F16 = mybir.dt.float16
BF16 = mybir.dt.bfloat16
ALU = mybir.AluOpType
ACT = mybir.ActivationFunctionType
AX_X = mybir.AxisListType.X

P = 128
B, L, D = 8, 1024, 128
FF = 512
NF = FF // P
S = 16
K = 3
GF = 336
GP = 112
NG = GF // GP
TILES = B * L // P
CH = L // P
T4 = 4
BT = T4 * P
NB = TILES // T4
DG = P // S
NGR = D // DG
TAB = NGR * P
HW = 2 * P
LN_EPS = 1e-5
RMS_EPS = 1e-6
MIX_C = 2 * D


def after(eng, sem, count):
    if not (isinstance(count, int) and count <= 0):
        eng.wait_ge(sem, count)


def each_block(eng, step, peel_front, peel_back=2):
    for i in range(peel_front):
        step(i, i % 2, i)
    with eng.Fori(peel_front // 2, (NB - peel_back) // 2) as pair:
        step(pair * 2, 0, None)
        step(pair * 2 + 1, 1, None)
    for i in range(NB - peel_back, NB):
        step(i, i % 2, i)


def macaron_kernel(nc, x, w1t, b1c, w2t, bias_rows, pre_w, wint, short_rows, short_x2, short_bc, poles, residues,
                   dskip, wot, post_w, l12t, l3t, out):
    with ExitStack() as ctx:
        def sb(name, shape, dt):
            return ctx.enter_context(nc.sbuf_tensor(name, shape, dt))

        def sem(name):
            return ctx.enter_context(nc.semaphore(name))

        xres = sb("xres", [P, TILES, D], F32)
        xv = sb("xv", [P, D, TILES], F32)
        x2T = sb("x2T", [P, B * L], F32)
        ring = sb("toeplitz_ring", [P, 4, DG, P], F32)
        vq = sb("vq_tables", [P, 2 * TAB], F32)
        ident = sb("ident", [P, P], F32)
        flip = sb("flip", [P, P], F32)
        ones_f = sb("ones_f", [P, P], F32)
        ones_b = sb("ones_b", [P, P], BF16)
        w1 = sb("w1", [P, FF], F16)
        w2 = sb("w2", [P, NF, D], F16)
        w2_last = sb("w2_last", [P, D], F32)
        b1 = sb("b1", [P, NF], F32)
        brow = sb("brow", [P, MIX_C + D], BF16)
        wk_hi = sb("wk_hi", [P, K, MIX_C], F16)
        wk_lo = sb("wk_lo", [P, K, MIX_C], F16)
        wx2_hi = sb("wx2_hi", [P, D], F16)
        wx2_lo = sb("wx2_lo", [P, D], F16)
        tap_x2 = sb("tap_x2", [P, K], F32)
        wo = sb("wo", [P, D], F32)
        l12_hi = sb("l12_hi", [P, 2 * NG, GP], F16)
        l12_lo = sb("l12_lo", [P, 2 * NG, GP], F16)
        l3_hi = sb("l3_hi", [GP, NG, D], F16)
        l3_lo = sb("l3_lo", [GP, NG, D], F16)
        sbx2 = sb("sbx2", [P, 1], F32)
        prew = sb("prew", [P, 1], F32)
        postw = sb("postw", [P, 1], F32)
        lp = sb("lp", [P, NGR], F32)
        res = sb("res", [P, NGR], F32)
        dsk = sb("dsk", [DG, NGR], F32)
        decay = sb("decay", [P, NGR], F32)
        rp = sb("rp", [P, NGR], F32)
        sel_res = sb("sel_res", [P, NGR, DG], F32)
        sel_rp = sb("sel_rp", [P, NGR, DG], F32)
        sel = sb("sel", [P, DG], F32)
        carry = sb("carry", [P, TILES], F32)
        mhalf = sb("mhalf", [P, 2, T4], F32)
        rms_eps = sb("rms_eps", [P, T4], F32)
        negm1 = sb("negm1", [P, TILES], F32)
        rstd1 = sb("rstd1", [P, TILES], F32)
        small = sb("small", [P, 8], F32)

        xn = sb("xn", [P, 2, T4, P], F32)
        xnT_hi = sb("xnT_hi", [P, 2, BT], F16)
        xnT_lo = sb("xnT_lo", [P, 2, BT], F16)
        h32 = sb("h32", [P, NF, BT], F32)
        h_hi = sb("h_hi", [P, 2, NF, BT], F16)
        h_lo = sb("h_lo", [P, 2, NF, BT], F16)
        bnst = sb("bnst", [P, 2, T4, 6], F32)
        mv = sb("mv", [P, 2, 6, T4], F32)
        fs = sb("fs", [P, 2, T4], F32)
        xin = sb("xin", [P, 2, T4, P], F32)
        xinT_hi = sb("xinT_hi", [P, 2 + L], F16)
        xinT_lo = sb("xinT_lo", [P, 2 + L], F16)
        bnst2 = sb("bnst2", [P, 2, T4, 6], F32)
        mv2 = sb("mv2", [P, 2, 8, T4], F32)
        ms = sb("ms", [P, 2, 2, T4], F32)
        x2_raw = sb("x2_raw", [P, 2 + L], F32)
        vt = sb("vt", [P, 2, 2, P], F32)
        qs = sb("qs", [P, 4, P], F32)
        vs = sb("vs", [P, 4, P], F32)
        ssum = sb("ssum", [P, 2, TILES], F32)
        dk = sb("dk", [P, 2, TILES], F32)
        state = sb("state", [P, 2, TILES], F32)
        ss = sb("ss", [P, 2, T4], F32)
        rr = sb("rr", [P, 2, 2, T4], F32)

        setup_a = x2T[:, :]
        w1s, w2s = setup_a[:, 0:512], setup_a[:, 512:1024]
        wins, srows = setup_a[:, 1024:1408], setup_a[:, 1408:1408 + K * MIX_C]
        l12s, brs = setup_a[:, 2560:3232], setup_a[:, 3232:3616]
        l3s = setup_a[0:GP, 3616:3616 + NG * D].rearrange("p (f d) -> p f d", f=NG)
        tmp_a, iota_t = setup_a[:, 6144:8192], setup_a[:, 4096:4096 + P]
        ring_flat = ring[:, :, :, :].rearrange("p a b c -> p (a b c)")
        hp = ring_flat[0:DG, 0:TAB]
        hp_pairs = ring_flat[0:DG, TAB:2 * TAB]
        hp_parts = hp_pairs.bitcast(F16).rearrange("p (t h) -> p t h", h=2)
        ring_parts = ring[:, :, :, :].bitcast(F16).rearrange("p s c (t h) -> p s c t h", h=2)
        zeros = state[:, :, :].rearrange("p a t -> p (a t)")
        xv_hi, xv_lo = (t[:, :, :, :].rearrange("p a b c -> p (a b c)").bitcast(F16).rearrange(
            "p (s t) -> p s t", s=4) for t in (xn, xin))
        pow_t, v_all = vq[:, 0:TAB], vq[:, TAB:2 * TAB]
        gm = h_hi[:, :, :, :].rearrange("p a b c -> p (a b c)").bitcast(F32).rearrange(
            "p (a d t) -> p a d t", a=4, d=DG)[:, 0:2]
        masked = h_lo[:, :, :, :].rearrange("p a b c -> p (a b c)").bitcast(F32).rearrange(
            "p (a d t) -> p a d t", a=4, d=DG)
        gg_hi, gg_lo = (ring_flat[0:GP, n * NG * BT:(n + 1) * NG * BT].bitcast(F16).rearrange(
            "p (a f t) -> p a f t", a=2, f=NG) for n in range(2))
        gg = h32[0:GP]
        yxT = ring_flat[:, 2 * NG * BT:2 * NG * BT + 2 * BT].rearrange("p (a t) -> p a t", a=2)
        u_sb = vq[:, 0:2 * BT].rearrange("p (a t d) -> p a t d", a=2, t=T4)
        y_sb = vq[:, 2 * BT:4 * BT].rearrange("p (a t d) -> p a t d", a=2, t=T4)
        g1 = vq[0:GP, 4 * BT:6 * BT].rearrange("p (a t) -> p a t", a=2)
        yst, zm, zT_hi, zT_lo = xin, xn, xnT_hi, xnT_lo

        h_last = x2T[:, 0:2 * BT].rearrange("p (a t) -> p a t", a=2)

        bank = [ctx.enter_context(nc.psum_tensor(f"bank{n}", [P, BT], F32)) for n in range(8)]
        ps_xnT, ps_up, ps_down, ps_inT = bank[0], bank[1:3], bank[3], bank[4]
        ps_mix, ps_x2 = bank[5:7], bank[7]
        ps_state, ps_conv = bank[0:2], bank[2:4]
        ps_yT, ps_proj, ps_l1, ps_zT, ps_l2, ps_l3 = bank[0], bank[1], bank[2:4], bank[4], bank[5:7], bank[7]
        ps_up2 = bank[1:3] + bank[5:7]

        hpad = nc.dram_tensor("impulse", [D, HW], F32, kind="Internal")

        poles_loaded, x1_loaded, ffn_w_loaded, small_w_loaded, mix_w_loaded, x_loaded = (
            sem("poles_loaded"), sem("x1_loaded"), sem("ffn_w_loaded"), sem("small_w_loaded"), sem("mix_w_loaded"),
            sem("x_loaded"))
        impulse_stored, out_stored = sem("impulse_stored"), sem("out_stored")
        toeplitz_loaded = [sem(f"toeplitz_loaded{s}") for s in range(4)]
        cleared, consts, sel_ready, zeros_ready = (
            sem("cleared"), sem("consts"), sem("sel_ready"), sem("zeros_ready"))
        abs_summed, abs_total, dve_step = sem("abs_summed"), sem("abs_total"), sem("dve_step")
        w1_ready, w2_ready, bias_ready, weights_ready = (
            sem("w1_ready"), sem("w2_ready"), sem("bias_ready"), sem("weights_ready"))
        skip_added, impulse_split = sem("skip_added"), sem("impulse_split")
        powers, sel_res_ready, impulse_mm, impulse_copied, impulse_ready, pow_T, v_ready = (
            sem("powers"), sem("sel_res_ready"), sem("impulse_mm"), sem("impulse_copied"), sem("impulse_ready"),
            sem("pow_T"), sem("v_ready"))
        ffn_square, mix_square = sem("ffn_square"), sem("mix_square")
        ffn_bn, ffn_stats, ffn_centred, ffn_normed = (
            sem("ffn_bn"), sem("ffn_stats"), sem("ffn_centred"), sem("ffn_normed"))
        ffn_T, ffn_hi, ffn_lo, up_done, gelu_done, hid_lo, down_done, resid_done = (
            sem("ffn_T"), sem("ffn_hi"), sem("ffn_lo"), sem("up_done"), sem("gelu_done"), sem("hid_lo"),
            sem("down_done"), sem("resid_done"))
        hid0_lo = sem("hid0_lo")
        hid_lo2 = sem("hid_lo2")
        w2_last_ready = sem("w2_last_ready")
        mix_kept = sem("mix_kept")
        mix_bn, mix_stats, mix_step, mix_normed, mix_T, mix_hi, mix_lo = (
            sem("mix_bn"), sem("mix_stats"), sem("mix_step"), sem("mix_normed"), sem("mix_T"), sem("mix_hi"),
            sem("mix_lo"))
        mix_mm, v_copied, xv_done, x2_mm, x2_stored, x2_tap, x2_done = (
            sem("mix_mm"), sem("v_copied"), sem("xv_done"), sem("x2_mm"), sem("x2_stored"), sem("x2_tap"),
            sem("x2_done"))
        gm_cleared, xv_split, xv_rest = sem("gm_cleared"), sem("xv_split"), sem("xv_rest")
        in_table, out_table, state_mm, masked_done, summed, decay_ready, scanned, carry_ready, conv_mm, y_stored = (
            sem("in_table"), sem("out_table"), sem("state_mm"), sem("masked_done"), sem("summed"), sem("decay_ready"),
            sem("scanned"), sem("carry_ready"), sem("conv_mm"), sem("y_stored"))
        y_staged, y_T, gated, proj_mm, u_centred, u_ready, y_sum, squared = (
            sem("y_staged"), sem("y_T"), sem("gated"), sem("proj_mm"), sem("u_centred"), sem("u_ready"),
            sem("y_sum"), sem("squared"))
        z_var, z_rstd, z_ready, xy_done, z_T, z_hi, z_lo = (
            sem("z_var"), sem("z_rstd"), sem("z_ready"), sem("xy_done"), sem("z_T"), sem("z_hi"), sem("z_lo"))
        l12_mm, g1_done, glu_done, glu_hi, glu_lo, l3_mm, mixed = (
            sem("l12_mm"), sem("g1_done"), sem("glu_done"), sem("glu_hi"), sem("glu_lo"), sem("l3_mm"), sem("mixed"))

        block = ctx.enter_context(nc.Block())

        def tiles_of(t, i):
            return t[:, bass.ds(i * T4, T4), :]

        def per_tile(stat):
            return stat.unsqueeze(2).to_broadcast([P, T4, D])

        @block.sync
        def _(sp):
            sp.dma_start(tiles_of(xres, 0), x[:, 0:T4, :]).then_inc(x_loaded, 16)
            sp.dma_start(lp[:], poles).then_inc(poles_loaded, 16)
            for dst, src in ((w1s, w1t), (w2s, w2t), (b1[:], b1c)):
                sp.dma_start(dst, src).then_inc(ffn_w_loaded, 16)
            sp.dma_start(tiles_of(xres, 1), x[:, T4:2 * T4, :]).then_inc(x1_loaded, 16)
            for dst, src in ((res[:], residues), (dsk[:], dskip), (brs, bias_rows)):
                sp.dma_start(dst, src).then_inc(small_w_loaded, 16)
            for dst, src in ((prew[:], pre_w), (wins, wint), (srows, short_rows), (tap_x2[:], short_x2),
                             (sbx2[:], short_bc), (wo[:], wot), (postw[:], post_w), (l12s, l12t), (l3s, l3t)):
                sp.dma_start(dst, src).then_inc(mix_w_loaded, 16)
            with sp.Fori(2, NB) as i:
                sp.wait_ge(x_loaded, i * 16 - 16)
                sp.dma_start(tiles_of(xres, i), x[:, bass.ds(i * T4, T4), :]).then_inc(x_loaded, 16)
            sp.wait_ge(zeros_ready, 1)
            sp.dma_start(hpad[:, P:HW], zeros).then_inc(impulse_stored, 16)
            sp.wait_ge(impulse_ready, 1)
            sp.dma_start(hpad[:, 0:P].rearrange("(g p) w -> p g w", p=DG),
                         hp_pairs.rearrange("p (g w) -> p g w", g=NGR)).then_inc(impulse_stored, 16)
            sp.wait_ge(impulse_stored, 32)
            for g in range(NGR):
                after(sp, conv_mm, g - 3)
                src = bass.AP(hpad, g * DG * HW, [[1, P], [HW, DG], [1, P]])
                sp.dma_start(ring[:, g % 4, :, :], src).then_inc(toeplitz_loaded[g % 4], 16)
            with sp.Fori(0, NB) as i:
                sp.wait_ge(resid_done, i + (NB + 1))
                sp.dma_start(out[:, bass.ds(i * T4, T4), :], tiles_of(xres, i)).then_inc(out_stored, 16)
            sp.wait_ge(out_stored, 16 * NB)

        @block.tensor
        def _(pe):
            pe.wait_ge(abs_summed, 1)
            pe.wait_ge(consts, 1)
            pe.matmul(ps_x2[:, 0:2], ones_f[:], small[:, 0:2], start=True, stop=True).then_inc(abs_total, 1)
            pe.wait_ge(sel_ready, 2)

            def impulse_responses():
                pe.wait_ge(powers, 1)
                pe.wait_ge(sel_res_ready, 1)
                for g in range(NGR):
                    last = pe.matmul(bank[4 + g // 4][0:DG, (g % 4) * P:(g % 4 + 1) * P], sel_res[:, g, :],
                                     pow_t[:, g * P:(g + 1) * P], start=True, stop=True)
                    if g % 4 == 3:
                        last.then_inc(impulse_mm, 1)

            def transpose_powers():
                for g in range(NGR):
                    if g % 4 == 0:
                        pe.wait_ge(impulse_copied, g // 4 + 1)
                    last = pe.transpose(bank[4 + g // 4][:, (g % 4) * P:(g % 4 + 1) * P],
                                        pow_t[:, g * P:(g + 1) * P], ident[:])
                    if g % 4 == 3:
                        last.then_inc(pow_T, 1)

            def ffn_transpose(n, par):
                pe.wait_ge(ffn_normed, n + 1)
                after(pe, ffn_lo, n)
                for t in range(T4):
                    last = pe.transpose(ps_xnT[:, t * P:(t + 1) * P], xn[:, par, t, :], ident[:])
                last.then_inc(ffn_T, 1)

            def ffn_up(n, par, f):
                if f == 0:
                    pe.wait_ge(ffn_lo, n + 1)
                after(pe, gelu_done, n * NF + f - 1)
                o = ps_up[f % 2][:]
                pe.matmul(o, w1[:, f * P:(f + 1) * P], xnT_hi[:, par, :], start=True, stop=False)
                pe.matmul(o, w1[:, f * P:(f + 1) * P], xnT_lo[:, par, :], start=False, stop=True)\
                    .then_inc(up_done, 1)

            def ffn_down(n, par):
                pe.wait_ge(hid_lo, n * (NF - 1) + (NF - 1))
                pe.wait_ge(hid0_lo, n + 1)
                after(pe, resid_done, n)
                for t in range(T4):
                    o = ps_down[:, t * P:(t + 1) * P]
                    pe.matmul(o, ones_b[:], brow[:, MIX_C:MIX_C + D], start=True, stop=False)
                    for f in range(NF):
                        cut = slice(t * P, (t + 1) * P)
                        pe.matmul(o, h_hi[:, par, f, cut], w2[:, f, :], start=False, stop=False)
                        last = pe.matmul(o, h_lo[:, par, f, cut], w2[:, f, :], start=False, stop=f == NF - 1)
                last.then_inc(down_done, 1)

            def ffn2_up(n, par, f):
                if f == 0:
                    pe.wait_ge(ffn_lo, n + 1)
                pe.wait_ge(gelu_done, n * NF + (f - (NF - 1)))
                o = ps_up2[f][:]
                pe.matmul(o, w1[:, f * P:(f + 1) * P], xnT_hi[:, par, :], start=True, stop=False)
                pe.matmul(o, w1[:, f * P:(f + 1) * P], xnT_lo[:, par, :], start=False, stop=True)\
                    .then_inc(up_done, 1)

            def ffn2_down(n, i, par, half):
                if half == 0:
                    pe.wait_ge(hid_lo2, i * (NF - 1) + (NF - 1))
                    pe.wait_ge(gelu_done, n * NF + NF)
                    pe.wait_ge(resid_done, n)
                for t in (2 * half, 2 * half + 1):
                    o = ps_down[:, t * P:(t + 1) * P]
                    cut = slice(t * P, (t + 1) * P)
                    pe.matmul(o, ones_b[:], brow[:, MIX_C:MIX_C + D], start=True, stop=False)
                    for f in range(NF - 1):
                        pe.matmul(o, h_hi[:, par, f, cut], w2[:, f, :], start=False, stop=False)
                        pe.matmul(o, h_lo[:, par, f, cut], w2[:, f, :], start=False, stop=False)
                    last = pe.matmul(o, h_last[:, par, cut], w2_last[:], start=False, stop=True)
                if half == 1:
                    last.then_inc(down_done, 1)

            def mix_transpose(i, par):
                pe.wait_ge(mix_normed, i + 1)
                after(pe, mix_lo, i)
                for t in range(T4):
                    last = pe.transpose(ps_inT[:, t * P:(t + 1) * P], xin[:, par, t, :], ident[:])
                last.then_inc(mix_T, 1)

            def mix_project(j, par, pair):
                if pair == 0:
                    pe.wait_ge(mix_lo, j + 1)
                after(pe, xv_done, j * 2 + (pair - 1))
                for a in range(2):
                    o = ps_mix[pair][:, a * MIX_C:(a + 1) * MIX_C]
                    pe.matmul(o, ones_b[:], brow[:, 0:MIX_C], start=True, stop=False)
                    for k in range(K):
                        at = par * BT + (2 * pair + a) * P + k
                        hi, lo = xinT_hi[:, at:at + P], xinT_lo[:, at:at + P]
                        pe.matmul(o, hi, wk_hi[:, k, :], start=False, stop=False)
                        pe.matmul(o, hi, wk_lo[:, k, :], start=False, stop=False)
                        last = pe.matmul(o, lo, wk_hi[:, k, :], start=False, stop=k == K - 1)
                last.then_inc(mix_mm, 1)

            def mix_project_x2(j, par):
                after(pe, x2_stored, j)
                cut = slice(2 + par * BT, 2 + (par + 1) * BT)
                pe.matmul(ps_x2[:], wx2_hi[:], xinT_hi[:, cut], start=True, stop=False)
                pe.matmul(ps_x2[:], wx2_hi[:], xinT_lo[:, cut], start=False, stop=False)
                pe.matmul(ps_x2[:], wx2_lo[:], xinT_hi[:, cut], start=False, stop=True).then_inc(x2_mm, 1)

            ffn_transpose(0, 0)
            pe.wait_ge(w1_ready, 1)

            def step(i, par, known):
                if known == 2:
                    pe.wait_ge(weights_ready, 2)
                    pe.wait_ge(v_ready, 4)
                ffn_up(i, par, 0)
                ffn_up(i, par, 1)
                if known is None or known >= 2:
                    mix_project(i - 2, par, 0)
                if known != NB - 1:
                    ffn_transpose(i + 1, 1 - par)
                ffn_up(i, par, 2)
                ffn_up(i, par, 3)
                if known is None or known >= 2:
                    mix_project_x2(i - 2, par)
                    mix_project(i - 2, par, 1)
                if known == 0:
                    pe.wait_ge(w2_ready, 1)
                    pe.wait_ge(bias_ready, 1)
                if known == 1:
                    impulse_responses()
                    transpose_powers()
                    pe.wait_ge(v_ready, 1)
                if known != 0:
                    mix_transpose(i - 1, 1 - par)
                ffn_down(i, par)

            each_block(pe, step, 4)
            for j in (NB - 2, NB - 1):
                if j == NB - 1:
                    mix_transpose(j, 1)
                mix_project(j, j % 2, 0)
                mix_project(j, j % 2, 1)
                mix_project_x2(j, j % 2)

            pe.wait_ge(xv_done, 2 * NB)
            pe.wait_ge(resid_done, NB)

            def group_rhs(g):
                return xv[:, bass.ds(g * DG, DG), :].rearrange("p a b -> p (a b)")

            def conv_state(g, s):
                pe.wait_ge(in_table, g + 1)
                after(pe, masked_done, g - 1)
                pe.matmul(ps_state[s % 2][:], vs[:, s, :], group_rhs(g), start=True, stop=True)\
                    .then_inc(state_mm, 1)

            def conv_from_states(g, s):
                pe.wait_ge(out_table, g + 1)
                pe.wait_ge(carry_ready, g + 1)
                after(pe, y_stored, g - 1)
                pe.matmul(ps_conv[s % 2][:], qs[:, s, :], gm[:, s % 2, :, :].rearrange("p d t -> p (d t)"),
                          start=True, stop=True, skip_group_check=True)

            def conv_in_chunk(g, s, turn):
                pe.wait_ge(xv_rest, g + 1)
                pe.wait_ge(toeplitz_loaded[s], turn * 16 + 16)
                for c in range(DG):
                    cut = slice(c * TILES, (c + 1) * TILES)
                    for matrix, rhs in ((0, xv_hi), (0, xv_lo), (1, xv_hi)):
                        last = pe.matmul(ps_conv[s % 2][:, cut], ring_parts[:, s, c, :, matrix], rhs[:, s, cut],
                                         start=False, stop=True, skip_group_check=True)
                last.then_inc(conv_mm, 1)

            def conv_turn(turn, last_turn=False):
                for s in range(4):
                    if not (last_turn and s >= 2):
                        conv_state(turn * 4 + (s + 2), (s + 2) % 4)
                    conv_from_states(turn * 4 + s, s)
                    conv_in_chunk(turn * 4 + s, s, turn)

            conv_state(0, 0)
            conv_state(1, 1)
            conv_turn(0)
            with pe.Fori(1, NGR // 4 - 1) as turn:
                conv_turn(turn)
            conv_turn(NGR // 4 - 1, True)

            def y_transpose(i, par):
                pe.wait_ge(y_staged, i + 1)
                after(pe, gated, i)
                for t in range(T4):
                    last = pe.transpose(ps_yT[:, t * P:(t + 1) * P], yst[:, par, t, :], flip[:])
                last.then_inc(y_T, 1)

            def project_out(i, par):
                pe.wait_ge(gated, i + 1)
                after(pe, y_sum, i)
                for t in range(T4):
                    last = pe.matmul(ps_proj[:, t * P:(t + 1) * P], yxT[:, par, t * P:(t + 1) * P], wo[:],
                                     start=True, stop=True)
                last.then_inc(proj_mm, 1)

            def z_transpose(i, par):
                pe.wait_ge(z_ready, i + 1)
                after(pe, z_lo, i)
                for t in range(T4):
                    last = pe.transpose(ps_zT[:, t * P:(t + 1) * P], zm[:, par, t, :], ident[:])
                last.then_inc(z_T, 1)

            def gate_up(i, par, f):
                if f == 0:
                    pe.wait_ge(z_lo, i + 1)
                b = (NG * par + f) % 2
                after(pe, glu_done, i * NG + (f - 1))
                for m, ps in ((f, ps_l1[b]), (NG + f, ps_l2[b])):
                    o = ps[0:GP, :]
                    pe.matmul(o, l12_hi[:, m, :], zT_hi[:, par, :], start=True, stop=False)
                    pe.matmul(o, l12_hi[:, m, :], zT_lo[:, par, :], start=False, stop=False)
                    last = pe.matmul(o, l12_lo[:, m, :], zT_hi[:, par, :], start=False, stop=True)
                last.then_inc(l12_mm, 1)

            def gate_down(i, par):
                pe.wait_ge(glu_lo, i * NG + NG)
                after(pe, mixed, i)
                for t in range(T4):
                    o, cut = ps_l3[:, t * P:(t + 1) * P], slice(t * P, (t + 1) * P)
                    for f in range(NG):
                        pe.matmul(o, gg_hi[:, par, f, cut], l3_hi[:, f, :], start=f == 0, stop=False)
                        pe.matmul(o, gg_hi[:, par, f, cut], l3_lo[:, f, :], start=False, stop=False)
                        last = pe.matmul(o, gg_lo[:, par, f, cut], l3_hi[:, f, :], start=False, stop=f == NG - 1)
                last.then_inc(l3_mm, 1)

            pe.wait_ge(masked_done, NGR)
            pe.wait_ge(y_stored, NGR)
            for i in range(2):
                y_transpose(i, i)
                project_out(i, i)
            z_transpose(0, 0)

            def step(i, par, known):
                gate_up(i, par, 0)
                if known is None or known < NB - 2:
                    y_transpose(i + 2, par)
                gate_up(i, par, 1)
                if known is None or known < NB - 2:
                    project_out(i + 2, par)
                if known != NB - 1:
                    z_transpose(i + 1, 1 - par)
                else:
                    ffn_transpose(NB, 0)
                if known != 0:
                    gate_down(i - 1, 1 - par)
                gate_up(i, par, 2)

            each_block(pe, step, 2)

            pe.wait_ge(w2_last_ready, 1)
            pe.wait_ge(y_sum, NB)

            def step(i, par, known):
                ffn2_up(i + NB, par, 0)
                if known == 0:
                    pe.wait_ge(glu_done, NG * NB)
                ffn2_up(i + NB, par, 1)
                if known != NB - 1:
                    ffn_transpose(i + (NB + 1), 1 - par)
                if known != 0:
                    ffn2_down(i + (NB - 1), i - 1, 1 - par, 0)
                ffn2_up(i + NB, par, 2)
                if known != 0:
                    ffn2_down(i + (NB - 1), i - 1, 1 - par, 1)
                ffn2_up(i + NB, par, 3)
                if known == 0:
                    gate_down(NB - 1, 1)

            each_block(pe, step, 2)
            for half in range(2):
                ffn2_down(2 * NB - 1, NB - 1, 1, half)

        @block.scalar
        def _(act):
            def pole_powers(g0, g1):
                for g in range(g0, g1):
                    act.activation(pow_t[:, g * P:(g + 1) * P], iota_t, ACT.Exp, scale=lp[:, g:g + 1])

            act.wait_ge(consts, 1)
            act.activation(small[:, 2:3], ones_f[:, 0:1], ACT.Exp)
            act.wait_ge(poles_loaded, 16)
            act.wait_ge(sel_ready, 2)
            pole_powers(0, 7)
            act.wait_ge(ffn_w_loaded, 48)
            act.activation(tmp_a[:, 0:FF], w1s, ACT.Abs, accum_out=small[:, 0:1])
            act.activation(tmp_a[:, FF:2 * FF], w2s, ACT.Abs, accum_out=small[:, 1:2]).then_inc(abs_summed, 1)
            pole_powers(7, NGR)
            act.activation(decay[:], lp[:], ACT.Exp, scale=float(P)).then_inc(powers, 1)

            def copy_impulse():
                for q in range(4):
                    act.wait_ge(impulse_mm, q + 1)
                    act.activation(hp[:, q * BT:(q + 1) * BT], bank[4 + q][0:DG, :], ACT.Copy)\
                        .then_inc(impulse_copied, 1)

            def copy_powers():
                for q in range(4):
                    act.wait_ge(pow_T, q + 1)
                    act.activation(v_all[:, q * BT:(q + 1) * BT], bank[4 + q][:], ACT.Copy).then_inc(v_ready, 1)

            def ffn_split_hi(n, par):
                act.wait_ge(ffn_T, n + 1)
                act.activation(xnT_hi[:, par, :], ps_xnT[:], ACT.Copy).then_inc(ffn_hi, 1)

            def ffn_gelu(n, par, f):
                act.wait_ge(up_done, n * NF + f + 1)
                if f == 0:
                    after(act, hid0_lo, n)
                else:
                    after(act, hid_lo, n * (NF - 1) + (f - (NF - 1)))
                act.activation(h32[:, f, :], ps_up[f % 2][:], ACT.Gelu, bias=b1[:, f:f + 1])
                act.activation(h_hi[:, par, f, :], ps_up[f % 2][:], ACT.Gelu, bias=b1[:, f:f + 1])\
                    .then_inc(gelu_done, 1)

            def mix_split_hi(i, par):
                act.wait_ge(mix_T, i + 1)
                act.activation(xinT_hi[:, 2 + par * BT:2 + (par + 1) * BT], ps_inT[:], ACT.Copy)\
                    .then_inc(mix_hi, 1)

            def copy_v(j, pair):
                act.wait_ge(mix_mm, j * 2 + (pair + 1))
                after(act, xv_done, j * 2 + (pair - 1))
                act.activation(vt[:, pair, :, :], ps_mix[pair][:].rearrange("p (a c) -> p a c", a=2)[:, :, D:2 * D],
                               ACT.Copy).then_inc(v_copied, 1)

            def store_x2(j, par):
                act.wait_ge(x2_mm, j + 1)
                after(act, x2_done, j - par)
                act.activation(x2_raw[:, 2 + par * BT:2 + (par + 1) * BT], ps_x2[:], ACT.Copy)
                act.activation(x2T[:, bass.ds(j * BT, BT)], ps_x2[:], ACT.Identity, bias=sbx2[:, 0:1],
                               scale=tap_x2[:, K - 1:K]).then_inc(x2_stored, 1)

            ffn_split_hi(0, 0)

            def step(i, par, known):
                ffn_gelu(i, par, 0)
                ffn_gelu(i, par, 1)
                if known is None or known >= 2:
                    copy_v(i - 2, 0)
                if known != NB - 1:
                    ffn_split_hi(i + 1, 1 - par)
                ffn_gelu(i, par, 2)
                ffn_gelu(i, par, 3)
                if known is None or known >= 2:
                    store_x2(i - 2, par)
                    copy_v(i - 2, 1)
                if known == 1:
                    copy_impulse()
                    copy_powers()
                if known != 0:
                    mix_split_hi(i - 1, 1 - par)
                if known == 1:
                    act.wait_ge(skip_added, 1)
                    act.activation(hp_parts[:, :, 0], hp, ACT.Copy).then_inc(impulse_split, 1)

            each_block(act, step, 4)
            for j in (NB - 2, NB - 1):
                if j == NB - 1:
                    mix_split_hi(j, 1)
                copy_v(j, 0)
                copy_v(j, 1)
                store_x2(j, j % 2)

            def store_y(g, s):
                act.wait_ge(conv_mm, g + 1)
                act.activation(xv[:, bass.ds(g * DG, DG), :],
                               ps_conv[s % 2][:].rearrange("p (c t) -> p c t", c=DG), ACT.Copy).then_inc(y_stored, 1)

            def split_xv_hi(g, s):
                act.activation(xv_hi[:, s, :], xv[:, bass.ds(g * DG, DG), :].rearrange("p a b -> p (a b)"),
                               ACT.Copy).then_inc(xv_split, 1)

            act.wait_ge(xv_done, 2 * NB)
            act.wait_ge(ffn_T, NB)
            act.wait_ge(mix_T, NB)
            for g in range(4):
                split_xv_hi(g, g)
            with act.Fori(0, NGR // 4 - 1) as turn:
                for s in range(4):
                    store_y(turn * 4 + s, s)
                    split_xv_hi(turn * 4 + (s + 4), s)
            for s in range(4):
                store_y(NGR - 4 + s, s)

            def square(i, par):
                act.wait_ge(y_sum, i + 1)
                after(act, z_T, i - 1)
                for t in range(T4):
                    last = act.activation(zm[:, par, t, :], y_sb[:, par, t, :], ACT.Square,
                                          scale=D ** -0.5, accum_out=ss[:, par, t:t + 1])
                last.then_inc(squared, 1)

            def z_split_hi(i, par):
                act.wait_ge(z_T, i + 1)
                act.activation(zT_hi[:, par, :], ps_zT[:], ACT.Copy).then_inc(z_hi, 1)

            def gate_gelu(i, par, f):
                b = (NG * par + f) % 2
                act.wait_ge(l12_mm, i * NG + (f + 1))
                after(act, glu_done, i * NG + (f - 1))
                act.activation(g1[:, b, :], ps_l1[b][0:GP, :], ACT.Gelu_apprx_tanh).then_inc(g1_done, 1)

            def gate_hi(i, par, f):
                act.wait_ge(glu_done, i * NG + (f + 1))
                after(act, l3_mm, i - 1)
                act.activation(gg_hi[:, par, f, :], gg[:, f, :], ACT.Copy).then_inc(glu_hi, 1)

            square(0, 0)
            z_split_hi(0, 0)
            square(1, 1)

            def step(i, par, known):
                if known != 0:
                    gate_hi(i - 1, 1 - par, 2)
                gate_gelu(i, par, 0)
                gate_gelu(i, par, 1)
                gate_hi(i, par, 0)
                if known != NB - 1:
                    z_split_hi(i + 1, 1 - par)
                else:
                    ffn_split_hi(NB, 0)
                if known is None or known < NB - 2:
                    square(i + 2, par)
                gate_gelu(i, par, 2)
                gate_hi(i, par, 1)

            each_block(act, step, 2)

            act.wait_ge(gated, NB)

            def ffn2_gelu(n, i, par, f, known):
                act.wait_ge(up_done, n * NF + f + 1)
                if f == NF - 1:
                    act.activation(h_last[:, par, :], ps_up2[f][:], ACT.Gelu, bias=b1[:, f:f + 1])\
                        .then_inc(gelu_done, 1)
                    return
                if known == 0:
                    act.wait_ge(glu_lo, (NB - 1) * NG + f + 1)
                else:
                    act.wait_ge(hid_lo2, i * (NF - 1) + (f - 2))
                act.activation(h32[:, f, :], ps_up2[f][:], ACT.Gelu, bias=b1[:, f:f + 1])
                act.activation(h_hi[:, par, f, :], ps_up2[f][:], ACT.Gelu, bias=b1[:, f:f + 1])\
                    .then_inc(gelu_done, 1)

            def step(i, par, known):
                ffn2_gelu(i + NB, i, par, 0, known)
                if known == 0:
                    gate_hi(NB - 1, 1, 2)
                ffn2_gelu(i + NB, i, par, 1, known)
                if known != NB - 1:
                    ffn_split_hi(i + (NB + 1), 1 - par)
                ffn2_gelu(i + NB, i, par, 2, known)
                ffn2_gelu(i + NB, i, par, 3, known)

            each_block(act, step, 2)

        @block.vector
        def _(dve):
            chain = [0]

            def link(ins):
                chain[0] += 1
                ins.then_inc(dve_step, 1)
                dve.wait_ge(dve_step, chain[0])

            dve.memset(ones_b[:], 1.0)
            dve.memset(ones_f[:], 1.0).then_inc(consts, 1)
            dve.memset(carry[:], 1.0)
            dve.memset(xinT_hi[:, 0:2], 0.0)
            dve.memset(xinT_lo[:, 0:2], 0.0)
            dve.memset(x2_raw[:, 0:2], 0.0)
            link(dve.memset(zeros, 0.0))
            dve.memset(carry[:].rearrange("p (b c) -> p b c", b=B)[:, :, 0:1], 0.0).then_inc(zeros_ready, 1)

            def ternary_weights():
                below = tmp_a[:, 2 * FF:4 * FF]
                dve.wait_ge(abs_total, 1)
                link(dve.tensor_scalar(small[:, 2:4], ps_x2[:, 0:2], 1.0 / (D * FF), 1e-8, ALU.mult, ALU.max))
                dve.tensor_scalar(small[:, 4:6], small[:, 2:4], 0.5, None, ALU.mult)
                link(dve.tensor_scalar(small[:, 6:8], small[:, 2:4], -0.5, None, ALU.mult))
                link(dve.tensor_scalar(below[:, 0:FF], w1s, small[:, 6:7], None, ALU.is_lt))
                dve.scalar_tensor_tensor(w1[:], w1s, small[:, 4:5], below[:, 0:FF], ALU.is_gt, ALU.subtract)\
                    .then_inc(w1_ready, 1)
                link(dve.tensor_scalar(below[:, FF:2 * FF], w2s, small[:, 7:8], None, ALU.is_lt))
                dve.scalar_tensor_tensor(w2[:].rearrange("p f d -> p (f d)"), w2s, small[:, 5:6],
                                         below[:, FF:2 * FF], ALU.is_gt, ALU.subtract).then_inc(w2_ready, 1)

            def bias_parts():
                nbr = MIX_C + D
                cols = iter(setup_a[:, 4608 + n * nbr:4608 + (n + 1) * nbr] for n in range(4))
                rest, acc, acc2 = next(cols), next(cols), next(cols)
                part = next(cols).bitcast(BF16)[:, 0:nbr]
                dve.wait_ge(small_w_loaded, 48)
                dve.wait_ge(sel_ready, 2)
                link(dve.tensor_copy(part, brs))
                dve.tensor_tensor(rest, brs, part, ALU.subtract)
                link(dve.tensor_scalar(acc, part, ident[:, 0:1], None, ALU.mult))
                link(dve.tensor_copy(part, rest))
                link(dve.tensor_tensor(rest, rest, part, ALU.subtract))
                link(dve.scalar_tensor_tensor(acc2, part, ident[:, 1:2], acc, ALU.mult, ALU.add))
                dve.scalar_tensor_tensor(brow[:], rest, ident[:, 2:3], acc2, ALU.mult, ALU.add)\
                    .then_inc(bias_ready, 1)

            def pole_weights():
                sel_rows = sel[:].unsqueeze(1).to_broadcast([P, NGR, DG])
                dve.tensor_tensor(sel_res[:], sel_rows, res[:].unsqueeze(2).to_broadcast([P, NGR, DG]), ALU.mult)\
                    .then_inc(sel_res_ready, 1)
                dve.wait_ge(powers, 1)
                pow3 = pow_t.rearrange("p (g t) -> p g t", g=NGR)
                link(dve.tensor_tensor(rp[:].unsqueeze(2), res[:].unsqueeze(2), pow3[:, :, P - 2:P - 1], ALU.mult))
                dve.tensor_tensor(sel_rp[:], sel_rows, rp[:].unsqueeze(2).to_broadcast([P, NGR, DG]), ALU.mult)

            def mixer_weights():
                wprime, wk = tmp_a[:, 0:3 * D], tmp_a[:, 512:512 + K * MIX_C]
                dve.wait_ge(mix_w_loaded, 9 * 16)
                link(dve.tensor_scalar(wprime, wins, prew[:, 0:1], None, ALU.mult))
                dve.tensor_copy(wx2_hi[:], wprime[:, 0:D])
                wk3 = wk.rearrange("p (k c) -> p k c", k=K)
                link(dve.tensor_tensor(wk3, wprime[:, D:3 * D].unsqueeze(1).to_broadcast([P, K, MIX_C]),
                                       srows.rearrange("p (k c) -> p k c", k=K), ALU.mult))
                dve.tensor_tensor(wx2_lo[:], wprime[:, 0:D], wx2_hi[:], ALU.subtract)
                link(dve.tensor_copy(wk_hi[:], wk3))
                dve.tensor_tensor(wk_lo[:], wk3, wk_hi[:], ALU.subtract).then_inc(weights_ready, 1)

            def mlp_weights():
                link(dve.tensor_scalar(l12s, l12s, postw[:, 0:1], None, ALU.mult))
                l12v = l12s.rearrange("p (m c) -> p m c", m=2 * NG)
                link(dve.tensor_copy(l12_hi[:], l12v))
                dve.tensor_tensor(l12_lo[:], l12v, l12_hi[:], ALU.subtract)
                link(dve.tensor_copy(l3_hi[:], l3s))
                dve.tensor_tensor(l3_lo[:], l3s, l3_hi[:], ALU.subtract).then_inc(weights_ready, 1)
                newest = hp.rearrange("p (g w) -> p g w", g=NGR)[:, :, P - 1:P]
                dve.wait_ge(impulse_copied, 4)
                dve.tensor_tensor(newest, newest, dsk[:].unsqueeze(2), ALU.add).then_inc(skip_added, 1)

            def split_impulse():
                dve.wait_ge(impulse_split, 1)
                dve.tensor_tensor(hp_parts[:, :, 1], hp, hp_parts[:, :, 0], ALU.subtract).then_inc(impulse_ready, 1)

            def stats(n, par, buf, agg, sems, tile_block, rms):
                half, square, out_sem = sems
                for t in range(T4):
                    last = dve.bn_stats(buf[:, par, t, 0:6], xres[:, bass.ds(tile_block * T4 + t, 1), :]
                                        .rearrange("p a d -> p (a d)"))
                last.then_inc(half, 1)
                b, m = buf[:, par], agg[:, par]
                dve.wait_ge(half, n + 1)
                dve.tensor_tensor(m[:, 2, :], b[:, :, 1], b[:, :, 4], ALU.add)
                dve.tensor_tensor(m[:, 3, :], b[:, :, 1], b[:, :, 4], ALU.subtract)
                if rms:
                    dve.tensor_tensor(m[:, 4, :], b[:, :, 2], b[:, :, 5], ALU.add).then_inc(square, 1)
                else:
                    dve.scalar_tensor_tensor(m[:, 4, :], b[:, :, 2], D * LN_EPS, b[:, :, 5], ALU.add, ALU.add)\
                        .then_inc(square, 1)
                steps = 3 if rms else 2
                dve.wait_ge(square, n * steps + 1)
                dve.tensor_scalar(m[:, 0, :], m[:, 2, :], -0.5, None, ALU.mult)
                dve.scalar_tensor_tensor(m[:, 5, :], m[:, 3, :], 0.25, m[:, 3, :], ALU.mult, ALU.mult)\
                    .then_inc(square, 1)
                dve.wait_ge(square, n * steps + 2)
                last = dve.scalar_tensor_tensor(m[:, 1, :], m[:, 4, :], 1.0 / D, m[:, 5, :], ALU.mult, ALU.add)
                if rms:
                    last.then_inc(square, 1)
                    dve.wait_ge(square, n * steps + 3)
                    dve.tensor_scalar(m[:, 6, :], m[:, 1, :], LN_EPS, None, ALU.add)
                    last = dve.tensor_scalar(m[:, 7, :], m[:, 1, :], 1.0 + RMS_EPS, RMS_EPS * LN_EPS, ALU.mult,
                                             ALU.add)
                last.then_inc(out_sem, 1)

            def ffn_stat(n, i, par):
                after(dve, ffn_normed, n - 1)
                stats(n, par, bnst, mv, (ffn_bn, ffn_square, ffn_stats), i, rms=False)

            def ffn_split_lo(n, par):
                dve.wait_ge(ffn_hi, n + 1)
                dve.tensor_tensor(xnT_lo[:, par, :], ps_xnT[:], xnT_hi[:, par, :], ALU.subtract).then_inc(ffn_lo, 1)

            def hidden_lo(n, par, f):
                dve.wait_ge(gelu_done, n * NF + f + 1)
                dve.tensor_tensor(h_lo[:, par, f, :], h32[:, f, :], h_hi[:, par, f, :], ALU.subtract)\
                    .then_inc(hid_lo, 1)

            def ffn_residual(n, i):
                dve.wait_ge(down_done, n + 1)
                xb = tiles_of(xres, i).rearrange("p t d -> p (t d)")
                dve.scalar_tensor_tensor(xb, ps_down[:], 0.5, xb, ALU.mult, ALU.add).then_inc(resid_done, 1)

            def mix_stat(i, par):
                stats(i, par, bnst2, mv2, (mix_bn, mix_square, mix_stats), i, rms=True)

            def mix_split_lo(i, par):
                dve.wait_ge(mix_hi, i + 1)
                cut = slice(2 + par * BT, 2 + (par + 1) * BT)
                dve.tensor_tensor(xinT_lo[:, cut], ps_inT[:], xinT_hi[:, cut], ALU.subtract).then_inc(mix_lo, 1)

            def gate_x1_v(j, pair):
                dve.wait_ge(v_copied, j * 2 + (pair + 1))
                dve.tensor_tensor(xv[:, :, bass.ds(j * T4 + 2 * pair, 2)],
                                  ps_mix[pair][:].rearrange("p (a c) -> p c a", a=2)[:, 0:D, :],
                                  vt[:, pair, :, :].rearrange("p a c -> p c a"), ALU.mult).then_inc(xv_done, 1)

            def filter_x2(j, par):
                now = x2T[:, bass.ds(j * BT, BT)]
                dve.wait_ge(x2_stored, j + 1)
                for k, done in ((1, x2_tap), (0, x2_done)):
                    at = par * BT + k
                    dve.scalar_tensor_tensor(now, x2_raw[:, at:at + BT], tap_x2[:, k:k + 1], now, ALU.mult, ALU.add)\
                        .then_inc(done, 1)
                    if k == 1:
                        dve.wait_ge(x2_tap, j + 1)

            dve.wait_ge(x_loaded, 16)
            ffn_stat(0, 0, 0)
            dve.wait_ge(x1_loaded, 16)
            ffn_stat(1, 1, 1)
            ternary_weights()
            ffn_split_lo(0, 0)
            bias_parts()

            def step(i, par, known):
                hidden_lo(i, par, 1)
                if known is None or known >= 2:
                    gate_x1_v(i - 2, 0)
                if known != NB - 1:
                    ffn_split_lo(i + 1, 1 - par)
                if known == 0:
                    hidden_lo(i, par, 2)
                    hidden_lo(i, par, 3)
                if known is None or known < NB - 2:
                    dve.wait_ge(x_loaded, i * 16 + 32)
                    ffn_stat(i + 2, i + 2, par)
                if known != 0:
                    hidden_lo(i, par, 2)
                    hidden_lo(i, par, 3)
                if known is None or known >= 2:
                    filter_x2(i - 2, par)
                    gate_x1_v(i - 2, 1)
                if known == 0:
                    pole_weights()
                    mixer_weights()
                if known == 1:
                    mlp_weights()
                if known != 0:
                    mix_split_lo(i - 1, 1 - par)
                ffn_residual(i, i)
                after(dve, mix_kept, i - 1)
                dve.wait_ge(resid_done, i + 1)
                dve.tensor_copy(mv2[:, par, 2, :], ones_f[:, 0:T4])
                mix_stat(i, par)

            each_block(dve, step, 4)
            for j in (NB - 2, NB - 1):
                if j == NB - 1:
                    mix_split_lo(j, 1)
                    split_impulse()
                gate_x1_v(j, 0)
                gate_x1_v(j, 1)
                if j == NB - 2:
                    filter_x2(j, 0)

            mask_cols = sel[:].unsqueeze(2).to_broadcast([P, DG, TILES])
            dve.wait_ge(hid_lo, (NF - 1) * NB)
            dve.wait_ge(hid0_lo, NB)
            dve.wait_ge(down_done, NB)
            dve.wait_ge(gm_cleared, 1)
            dve.wait_ge(impulse_stored, 32)

            def mask_states(g, s):
                dve.tensor_scalar(dk[:, s, :], carry[:], decay[:, bass.ds(g, 1)], None, ALU.mult)\
                    .then_inc(decay_ready, 1)
                dve.wait_ge(state_mm, g + 1)
                dve.tensor_tensor(masked[:, s], ps_state[s][:].rearrange("p (c t) -> p c t", c=DG), mask_cols,
                                  ALU.mult)\
                    .then_inc(masked_done, 1)

            def sum_states(g, s):
                dve.wait_ge(masked_done, g + 1)
                dve.tensor_reduce(ssum[:, s, :], masked[:, s].rearrange("p c t -> p t c"), AX_X, ALU.add)\
                    .then_inc(summed, 1)

            def scan_states(g, s):
                dve.wait_ge(summed, g + 1)
                dve.wait_ge(decay_ready, g + 1)
                dve.tensor_tensor_scan(state[:, s, :], dk[:, s, :], ssum[:, s, :], 0.0, ALU.mult, ALU.add)\
                    .then_inc(scanned, 1)

            def spread_states(g, s):
                dve.wait_ge(scanned, g + 1)
                after(dve, conv_mm, g - 1)
                before = state[:, s, :].rearrange("p (b c) -> p b c", b=B)[:, :, 0:CH - 1]
                rp_cols = sel_rp[:, bass.ds(g, 1), :].rearrange("p a c -> p (a c)")
                into = gm[:, s, :, :].rearrange("p d (b c) -> p d b c", b=B)[:, :, :, 1:CH]
                dve.tensor_tensor(into, before.unsqueeze(1).to_broadcast([P, DG, B, CH - 1]),
                                  rp_cols.unsqueeze(2).unsqueeze(3).to_broadcast([P, DG, B, CH - 1]), ALU.mult)\
                    .then_inc(carry_ready, 1)

            def carry_states(g, s, last=False):
                if not last:
                    mask_states(g + 1, 1 - s)
                scan_states(g, s)
                if not last:
                    sum_states(g + 1, 1 - s)
                spread_states(g, s)

            mask_states(0, 0)
            sum_states(0, 0)
            for g in range(2):
                carry_states(g, g)
            filter_x2(NB - 1, 1)
            with dve.Fori(1, NGR // 2 - 1) as turn:
                for s in range(2):
                    carry_states(turn * 2 + s, s)
            for s in range(2):
                carry_states(NGR - 2 + s, s, last=s == 1)

            def stage_y(i, par):
                after(dve, y_T, i - 1)
                dve.tensor_copy(yst[:, par, :, :], xv[:, :, bass.ds(i * T4, T4)].rearrange("p d t -> p t d"))\
                    .then_inc(y_staged, 1)

            def gate_y(i, par):
                dve.wait_ge(y_T, i + 1)
                after(dve, proj_mm, i - 1)
                dve.tensor_tensor(yxT[:, par, :], ps_yT[:], x2T[:, bass.ds(i * BT, BT)], ALU.mult)\
                    .then_inc(gated, 1)

            def sum_y(i, par):
                dve.wait_ge(proj_mm, i + 1)
                dve.wait_ge(u_ready, i + 1)
                after(dve, xy_done, i - 1)
                dve.tensor_tensor(y_sb[:, par, :, :], ps_proj[:].rearrange("p (t d) -> p t d", t=T4),
                                  u_sb[:, par, :, :], ALU.add).then_inc(y_sum, 1)

            def z_split_lo(i, par):
                dve.wait_ge(z_hi, i + 1)
                dve.tensor_tensor(zT_lo[:, par, :], ps_zT[:], zT_hi[:, par, :], ALU.subtract).then_inc(z_lo, 1)

            def glu(i, par, f):
                b = (NG * par + f) % 2
                dve.wait_ge(g1_done, i * NG + (f + 1))
                after(dve, glu_lo, i * NG + (f - NG + 1))
                dve.tensor_tensor(gg[:, f, :], ps_l2[b][0:GP, :], g1[:, b, :], ALU.mult).then_inc(glu_done, 1)

            def gate_lo(i, par, f):
                dve.wait_ge(glu_hi, i * NG + (f + 1))
                dve.tensor_tensor(gg_lo[:, par, f, :], gg[:, f, :], gg_hi[:, par, f, :], ALU.subtract)\
                    .then_inc(glu_lo, 1)

            def mixer_residual(i):
                dve.wait_ge(l3_mm, i + 1)
                dve.wait_ge(xy_done, i + 1)
                xb = tiles_of(xres, i).rearrange("p t d -> p (t d)")
                dve.tensor_tensor(xb, ps_l3[:], xb, ALU.add).then_inc(mixed, 1)

            dve.wait_ge(y_stored, NGR)
            stage_y(0, 0)
            stage_y(1, 1)
            for i in range(2):
                gate_y(i, i)
                sum_y(i, i)
            stage_y(2, 0)
            z_split_lo(0, 0)

            def step(i, par, known):
                if known is None or known < NB - 2:
                    gate_y(i + 2, par)
                if known != 0:
                    gate_lo(i - 1, 1 - par, 2)
                glu(i, par, 0)
                if known is None or known < NB - 3:
                    stage_y(i + 3, 1 - par)
                glu(i, par, 1)
                gate_lo(i, par, 0)
                if known is None or known < NB - 2:
                    sum_y(i + 2, par)
                if known != NB - 1:
                    z_split_lo(i + 1, 1 - par)
                else:
                    ffn_split_lo(NB, 0)
                if known != 0:
                    mixer_residual(i - 1)
                if known in (NB - 3, NB - 2, NB - 1):
                    dve.wait_ge(mixed, 3)
                    ffn_stat(i + 3, i - (NB - 3), 1 - par)
                glu(i, par, 2)
                gate_lo(i, par, 1)

            each_block(dve, step, 2, 4)

            ffn_stat(NB + 3, 3, 1)

            def hidden_lo2(n, par, f):
                dve.wait_ge(gelu_done, n * NF + f + 1)
                dve.tensor_tensor(h_lo[:, par, f, :], h32[:, f, :], h_hi[:, par, f, :], ALU.subtract)\
                    .then_inc(hid_lo2, 1)

            def step(i, par, known):
                hidden_lo2(i + NB, par, 0)
                if known == 0:
                    gate_lo(NB - 1, 1, 2)
                if known != NB - 1:
                    ffn_split_lo(i + (NB + 1), 1 - par)
                hidden_lo2(i + NB, par, 1)
                if known != 0:
                    ffn_residual(i + (NB - 1), i - 1)
                hidden_lo2(i + NB, par, 2)
                if known == 0:
                    mixer_residual(NB - 1)
                if known is None or known < NB - 4:
                    dve.wait_ge(mixed, i + 5)
                    ffn_stat(i + (NB + 4), i + 4, par)

            each_block(dve, step, 2, 4)
            ffn_residual(2 * NB - 1, NB - 1)

        @block.gpsimd
        def _(pool):
            pool.memset(mhalf[:], -0.5)
            pool.memset(rms_eps[:], RMS_EPS)
            pool.memset(sel[:], 1.0)
            pool.memset(flip[:], 0.0)
            pool.memset(ident[:], 0.0).then_inc(cleared, 1)
            pool.wait_ge(cleared, 1)
            pool.affine_select(ident[:], ident[:], pattern=[[-1, P]], compare_op=ALU.not_equal, fill=1.0,
                               base=0, channel_multiplier=1)
            pool.affine_select(flip[:], flip[:], pattern=[[1, P]], compare_op=ALU.not_equal, fill=1.0,
                               base=1 - P, channel_multiplier=1)
            pool.iota(iota_t, pattern=[[-1, P]], base=P - 1, channel_multiplier=0, allow_small_or_imprecise_dtypes=True)
            pool.affine_select(sel[:], sel[:], pattern=[[-S, DG]], compare_op=ALU.is_ge, fill=0.0,
                               base=0, channel_multiplier=1).then_inc(sel_ready, 1)
            pool.wait_ge(sel_ready, 1)
            pool.affine_select(sel[:], sel[:], pattern=[[S, DG]], compare_op=ALU.is_ge, fill=0.0,
                               base=S - 1, channel_multiplier=-1).then_inc(sel_ready, 1)

            def ffn_norm(n, i, par):
                pool.wait_ge(ffn_stats, n + 1)
                after(pool, ffn_T, n - 1)
                pool.tensor_tensor(fs[:, par, :], mv[:, par, 1, :], mhalf[:, 0, :], ALU.pow)
                pool.tensor_tensor(xn[:, par, :, :], tiles_of(xres, i), per_tile(mv[:, par, 0, :]), ALU.add)\
                    .then_inc(ffn_centred, 1)
                pool.wait_ge(ffn_centred, n + 1)
                pool.tensor_tensor(xn[:, par, :, :], xn[:, par, :, :], per_tile(fs[:, par, :]), ALU.mult)\
                    .then_inc(ffn_normed, 1)

            def mix_norm(i, par):
                cols = bass.ds(i * T4, T4)
                negm = mv2[:, par, 0, :]
                pool.wait_ge(mix_stats, i + 1)
                after(pool, mix_T, i - 1)
                pool.tensor_tensor(ms[:, par, :, :], mv2[:, par, 6:8, :], mhalf[:], ALU.pow)
                pool.tensor_tensor(xin[:, par, :, :], tiles_of(xres, i), per_tile(negm), ALU.add).then_inc(mix_step, 1)
                pool.wait_ge(mix_step, i + 1)
                pool.tensor_tensor(xin[:, par, :, :], xin[:, par, :, :], per_tile(ms[:, par, 1, :]), ALU.mult)\
                    .then_inc(mix_normed, 1)
                pool.tensor_copy(negm1[:, cols], negm)
                pool.tensor_copy(rstd1[:, cols], ms[:, par, 0, :]).then_inc(mix_kept, 1)

            def hidden0_lo(n, par):
                pool.wait_ge(gelu_done, n * NF + 1)
                pool.tensor_tensor(h_lo[:, par, 0, :], h32[:, 0, :], h_hi[:, par, 0, :], ALU.subtract)\
                    .then_inc(hid0_lo, 1)

            ffn_norm(0, 0, 0)
            ffn_norm(1, 1, 1)
            pool.wait_ge(w2_ready, 1)
            pool.tensor_copy(w2_last[:], w2[:, NF - 1, :]).then_inc(w2_last_ready, 1)

            def step(i, par, known):
                hidden0_lo(i, par)
                if known != 0:
                    mix_norm(i - 1, 1 - par)
                if known is None or known < NB - 2:
                    ffn_norm(i + 2, i + 2, par)

            each_block(pool, step, 4)
            mix_norm(NB - 1, 1)

            def stage_in_table(g, s):
                after(pool, state_mm, g - 3)
                pool.tensor_copy(vs[:, s, :], v_all[:, bass.ds(g * P, P)]).then_inc(in_table, 1)

            def stage_out_table(g, s):
                after(pool, conv_mm, g - 3)
                pool.tensor_copy(qs[:, s, :], pow_t[:, bass.ds(g * P, P)]).then_inc(out_table, 1)

            def split_xv_lo(g, s):
                pool.tensor_tensor(xv_lo[:, s, :], xv[:, bass.ds(g * DG, DG), :].rearrange("p a b -> p (a b)"),
                                   xv_hi[:, s, :], ALU.subtract).then_inc(xv_rest, 1)

            pool.wait_ge(powers, 1)
            pool.wait_ge(v_ready, 4)
            for g in range(4):
                stage_in_table(g, g)
                stage_out_table(g, g)
            pool.wait_ge(hid_lo, (NF - 1) * NB)
            pool.wait_ge(down_done, NB)
            pool.memset(gm, 0.0).then_inc(gm_cleared, 1)
            pool.wait_ge(mix_T, NB)
            for g in range(4):
                pool.wait_ge(xv_split, g + 1)
                split_xv_lo(g, g)
            stage_in_table(4, 0)

            def stage_turn(turn, last_turn=False):
                for s in range(4):
                    g = turn * 4 + s
                    pool.wait_ge(xv_split, g + 1)
                    stage_out_table(g, s)
                    split_xv_lo(g, s)
                    if not (last_turn and s == 3):
                        stage_in_table(g + 1, (s + 1) % 4)

            with pool.Fori(1, NGR // 4 - 1) as turn:
                stage_turn(turn)
            stage_turn(NGR // 4 - 1, True)

            def make_u(i, par):
                cols = bass.ds(i * T4, T4)
                after(pool, y_sum, i - 1)
                pool.tensor_tensor(u_sb[:, par, :, :], tiles_of(xres, i), per_tile(negm1[:, cols]), ALU.add)\
                    .then_inc(u_centred, 1)
                pool.wait_ge(u_centred, i + 1)
                pool.tensor_tensor(u_sb[:, par, :, :], u_sb[:, par, :, :], per_tile(rstd1[:, cols]), ALU.mult)\
                    .then_inc(u_ready, 1)

            def z_norm(i, par):
                pool.wait_ge(squared, i + 1)
                pool.tensor_tensor(rr[:, par, 0, :], ss[:, par, :], rms_eps[:], ALU.add).then_inc(z_var, 1)
                pool.wait_ge(z_var, i + 1)
                pool.tensor_tensor(rr[:, par, 1, :], rr[:, par, 0, :], mhalf[:, 0, :], ALU.pow).then_inc(z_rstd, 1)
                pool.wait_ge(z_rstd, i + 1)
                pool.tensor_tensor(zm[:, par, :, :], y_sb[:, par, :, :], per_tile(rr[:, par, 1, :]), ALU.mult)\
                    .then_inc(z_ready, 1)
                pool.tensor_tensor(tiles_of(xres, i), tiles_of(xres, i), y_sb[:, par, :, :], ALU.add)\
                    .then_inc(xy_done, 1)

            pool.wait_ge(out_table, NGR)
            pool.wait_ge(state_mm, NGR)
            pool.wait_ge(mix_kept, NB)
            make_u(0, 0)
            make_u(1, 1)
            z_norm(0, 0)
            z_norm(1, 1)
            make_u(2, 0)

            def step(i, par, known):
                if known is None or known < NB - 3:
                    make_u(i + 3, 1 - par)
                if known is None or known < NB - 2:
                    z_norm(i + 2, par)

            each_block(pool, step, 2, 4)

            pool.wait_ge(z_T, NB - 1)
            ffn_norm(NB, 0, 0)
            pool.wait_ge(z_T, NB)
            ffn_norm(NB + 1, 1, 1)

            def step(i, par, known):
                if known is None or known < NB - 2:
                    ffn_norm(i + (NB + 2), i + 2, par)

            each_block(pool, step, 2)


def kernel(**inputs):
    import numpy as np
    import concourse.bacc as _bacc
    from concourse.bass_utils import run_bass_kernel_spmd as _run

    def arr(name):
        return np.asarray(inputs["L0_" + name])

    def rows(a):
        return np.broadcast_to(a.reshape(1, -1), (P, a.size))

    short = arr("attn_short_w").reshape(3 * D, K)
    short_b, b2 = arr("attn_short_b"), arr("ffn_b2")
    l12 = np.concatenate([arr("attn_l1_w"), arr("attn_l2_w")], axis=0)
    data = {
        "x": arr("attn_u").reshape(TILES, P, D).transpose(1, 0, 2),
        "w1t": arr("ffn_W1").T,
        "b1c": arr("ffn_b1").reshape(NF, P).T,
        "w2t": arr("ffn_W2").T.reshape(NF, P, D).transpose(1, 0, 2).reshape(P, NF * D),
        "bias_rows": rows(np.concatenate([short_b[D:], b2])),
        "pre_w": arr("attn_pre_norm_w").reshape(P, 1),
        "wint": arr("attn_in_proj_w").T,
        "short_rows": rows(short[D:].T),
        "short_x2": short[:D],
        "short_bc": short_b[:D].reshape(P, 1),
        "poles": arr("attn_log_poles").reshape(NGR, P).T,
        "residues": arr("attn_residues").reshape(NGR, P).T,
        "dskip": arr("attn_D_skip").reshape(NGR, DG).T,
        "wot": arr("attn_out_proj_w").T,
        "post_w": arr("attn_post_norm_w").reshape(P, 1),
        "l12t": l12.T,
        "l3t": arr("attn_l3_w").T.reshape(NG, GP, D).transpose(1, 0, 2),
    }
    nc = _bacc.Bacc("TRN2", target_bir_lowering=False, num_devices=1)
    arrays, args = {}, []
    for name, a in data.items():
        arrays[name] = np.ascontiguousarray(a)
        args.append(nc.dram_tensor(name, a.shape, F32, kind="ExternalInput").ap())
    args.append(nc.dram_tensor("out", (P, TILES, D), F32, kind="ExternalOutput").ap())
    macaron_kernel(nc, *args)
    r = _run(nc, [arrays], core_ids=[0])
    got = np.asarray(r.results[0]["out"])
    return np.ascontiguousarray(got.transpose(1, 0, 2)).reshape(B, L, D)
```
